# Optimizing a Trainium2 kernel written in Bass

```python
import numpy as np
import jax
import jax.numpy as jnp

def _softmax(x, axis=-1):
    return jax.nn.softmax(x, axis=axis)

def _gelu(x):
    return jax.nn.gelu(x, approximate=True)

def _silu(x):
    return jax.nn.silu(x)

def _sigmoid(x):
    return jax.nn.sigmoid(x)

def _layernorm(x, axis=-1, eps=1e-05):
    m = jnp.mean(x, axis=axis, keepdims=True)
    v = jnp.var(x, axis=axis, keepdims=True)
    return (x - m) / jnp.sqrt(v + eps)

def _scatter_add(tgt, idx, src, axis=0):
    return tgt.at[idx].add(src)

def _segment_sum(src, seg, n):
    return jax.ops.segment_sum(src, seg, n)
kernel_name = 'mk_adaln_ffn_d1_seqx_r8_a5725b'

def setup_inputs(seed: int=0):
    np.random.seed(seed)
    _w = jnp.asarray

    def _rec_inputs():
        import jax
        import jax.numpy as jnp
        _rk = jax.random.key(seed)
        x = -0.000125 + 0.9999 * jax.random.normal(jax.random.fold_in(_rk, 1), (32, 128, 128), jnp.float32)
        _lenS = 128 - jax.random.randint(jax.random.fold_in(_rk, 7), (32,), 0, max(1, 128 // 4) + 1, jnp.int32)
        _lenS2 = 128 - jax.random.randint(jax.random.fold_in(_rk, 8), (32,), 0, max(1, 128 // 4) + 1, jnp.int32)
        cond_1024 = -0.00493535 + 1.00056 * jax.random.normal(jax.random.fold_in(_rk, 11), (32, 128), jnp.float32)
        return (x, cond_1024)
    x, cond_1024 = _rec_inputs()

    def _L0_cond_setup():
        import jax, jax.numpy as jnp
        import numpy as np
        import math
        N, T, D, H = (64, 64, 128, 128)
        key = jax.random.key(seed)
        k1, k2, k3, k4 = jax.random.split(key, 4)
        x = jax.random.normal(k1, (N, T, D), dtype=jnp.float32)
        h0 = jax.random.normal(k2, (N, H), dtype=jnp.float32)
        Wx = jax.random.normal(k3, (D, 4 * H), dtype=jnp.float32) / math.sqrt(D)
        Wh = jax.random.normal(k4, (H, 4 * H), dtype=jnp.float32) / math.sqrt(H)
        b = jnp.zeros((4 * H,), dtype=jnp.float32)
        return {'x': x, 'h0': h0, 'Wx': Wx, 'Wh': Wh, 'b': b}
    _L0_cond_all = _L0_cond_setup()
    _L0_cond_in = {k: v for k, v in _L0_cond_all.items() if k in ('Wx', 'Wh', 'b')}
    del _L0_cond_all

    def _L0_ffn_setup():
        import jax, jax.numpy as jnp
        import numpy as np
        D, H, O, E, TOPK = (128, 512, 128, 8, 2)
        B, S = (4, 128)
        key = jax.random.key(seed)
        ks = jax.random.split(key, 12)
        std = 0.02
        return {'hidden_states': jax.random.normal(ks[0], (B, S, D), dtype=jnp.float32), 'norm_weight': jnp.ones((D,), dtype=jnp.float32), 'router_w': jax.random.normal(ks[1], (E, D), dtype=jnp.float32) * std, 'sw1': jax.random.normal(ks[2], (D, H), dtype=jnp.float32) * (1.0 / np.sqrt(D)), 'sb1': jnp.zeros((H,), dtype=jnp.float32), 'sw2': jax.random.normal(ks[3], (H, O), dtype=jnp.float32) * (1.0 / np.sqrt(H)), 'sb2': jnp.zeros((O,), dtype=jnp.float32), 'ew1': jax.random.normal(ks[4], (E, D, H), dtype=jnp.float32) * (1.0 / np.sqrt(D)), 'eb1': jnp.zeros((E, H), dtype=jnp.float32), 'ew2': jax.random.normal(ks[5], (E, H, O), dtype=jnp.float32) * (1.0 / np.sqrt(H)), 'eb2': jnp.zeros((E, O), dtype=jnp.float32)}
    _L0_ffn_all = _L0_ffn_setup()
    _L0_ffn_in = {k: v for k, v in _L0_ffn_all.items() if k in ('norm_weight', 'router_w', 'sw1', 'sb1', 'sw2', 'sb2', 'ew1', 'eb1', 'ew2', 'eb2')}
    del _L0_ffn_all
    return {'x': x, 'cond_1024': cond_1024, 'L0_cond_Wx': _L0_cond_in['Wx'], 'L0_cond_Wh': _L0_cond_in['Wh'], 'L0_cond_b': _L0_cond_in['b'], 'L0_ffn_norm_weight': _L0_ffn_in['norm_weight'], 'L0_ffn_router_w': _L0_ffn_in['router_w'], 'L0_ffn_sw1': _L0_ffn_in['sw1'], 'L0_ffn_sb1': _L0_ffn_in['sb1'], 'L0_ffn_sw2': _L0_ffn_in['sw2'], 'L0_ffn_sb2': _L0_ffn_in['sb2'], 'L0_ffn_ew1': _L0_ffn_in['ew1'], 'L0_ffn_eb1': _L0_ffn_in['eb1'], 'L0_ffn_ew2': _L0_ffn_in['ew2'], 'L0_ffn_eb2': _L0_ffn_in['eb2']}

def reference(x, cond_1024, L0_cond_Wx, L0_cond_Wh, L0_cond_b, L0_ffn_norm_weight, L0_ffn_router_w, L0_ffn_sw1, L0_ffn_sb1, L0_ffn_sw2, L0_ffn_sb2, L0_ffn_ew1, L0_ffn_eb1, L0_ffn_ew2, L0_ffn_eb2):
    import jax
    import jax.numpy as jnp

    def _L0_cond_ref(x, h0, Wx, Wh, b):
        import jax, jax.numpy as jnp
        import numpy as np
        import math
        N, T, D, H = (64, 64, 128, 128)
        Hdim = h0.shape[1]
        c0 = jnp.zeros_like(h0)
        xW = jnp.einsum('ntd,dk->tnk', x, Wx) + b

        def step(carry, xw_t):
            prev_h, prev_c = carry
            a = xw_t + prev_h @ Wh
            i = jax.nn.sigmoid(a[:, :Hdim])
            f = jax.nn.sigmoid(a[:, Hdim:2 * Hdim])
            o = jax.nn.sigmoid(a[:, 2 * Hdim:3 * Hdim])
            g = jnp.tanh(a[:, 3 * Hdim:])
            next_c = f * prev_c + i * g
            next_h = o * jnp.tanh(next_c)
            return ((next_h, next_c), next_h)
        _, hs = jax.lax.scan(step, (h0, c0), xW)
        return jnp.transpose(hs, (1, 0, 2))

    def _L0_ffn_ref(hidden_states, norm_weight, router_w, sw1, sb1, sw2, sb2, ew1, eb1, ew2, eb2):
        import jax, jax.numpy as jnp
        import numpy as np
        D, H, O, E, TOPK = (128, 512, 128, 8, 2)
        B, S = (4, 128)
        b, s, d = hidden_states.shape
        var = jnp.mean(jnp.square(hidden_states), axis=-1, keepdims=True)
        normed = hidden_states * jax.lax.rsqrt(var + 1e-08) * norm_weight
        shared = jnp.maximum(normed @ sw1 + sb1, 0.0) @ sw2 + sb2
        flat = normed.reshape(-1, d)
        T = flat.shape[0]
        probs = jax.nn.sigmoid(flat @ router_w.T)
        scores, idx = jax.lax.top_k(probs, TOPK)
        w = scores / (jnp.sum(scores, axis=-1, keepdims=True) + 1e-06)
        comb = jnp.zeros((T, E), dtype=flat.dtype)
        comb = comb.at[jnp.arange(T)[:, None], idx].add(w)
        h = jnp.maximum(jnp.einsum('td,edh->teh', flat, ew1) + eb1[None, :, :], 0.0)
        eo = jnp.einsum('teh,eho->teo', h, ew2) + eb2[None, :, :]
        routed = jnp.einsum('teo,te->to', eo, comb)
        return shared + routed.reshape(b, s, -1)
    x = x + _L0_ffn_ref(_L0_cond_ref(x, cond_1024, L0_cond_Wx, L0_cond_Wh, L0_cond_b), L0_ffn_norm_weight, L0_ffn_router_w, L0_ffn_sw1, L0_ffn_sb1, L0_ffn_sw2, L0_ffn_sb2, L0_ffn_ew1, L0_ffn_eb1, L0_ffn_ew2, L0_ffn_eb2)
    return x

_drawn_inputs = setup_inputs


def setup_inputs(seed=0):
    import zlib

    import numpy as np

    out = dict(_drawn_inputs(seed))
    spreads = {'L0_cond_b': (0.0, 0.1),
     'L0_ffn_norm_weight': (1.0, 0.2),
     'L0_ffn_sb1': (0.0, 0.1),
     'L0_ffn_sb2': (0.0, 0.1),
     'L0_ffn_eb1': (0.0, 0.1),
     'L0_ffn_eb2': (0.0, 0.1)}
    factors = {}
    for name, (base, spread) in spreads.items():
        noise = np.random.default_rng([zlib.crc32(name.encode()), seed]).standard_normal(out[name].shape)
        drawn = base * np.exp(spread * noise) if base else spread * noise
        out[name] = jnp.asarray(drawn.astype(out[name].dtype))
    for name, factor in factors.items():
        out[name] = (out[name] * factor).astype(out[name].dtype)
    return out
```

```python
import concourse.bass as bass
from concourse import mybir
from contextlib import ExitStack

F32 = mybir.dt.float32
F32R = mybir.dt.float32r
ALU = mybir.AluOpType
ACT = mybir.ActivationFunctionType
AX = mybir.AxisListType

N = 32
T = 128
D = 128
HID = 512
E = 8
X = E + 1
KT = HID // 128
GATES = 4
GS = 128 // N
STEPS = 16
TOK = STEPS * N
NG = STEPS // GS
CHUNKS = T // STEPS
TILES = X * KT
LEAD = 2
LAG = 2
ZB = 3
RING = 4
EPS_RMS = 1e-8
EPS_TOP = 1e-6

ROW_B1 = 0
ROW_B2 = ROW_B1 + TILES
ROW_NW = ROW_B2 + X
ROW_RW = ROW_NW + 1
ROW_H0 = ROW_RW + E
ROWS = ROW_H0 + N


def wait(eng, sem, value):
    if not isinstance(value, int) or value > 0:
        eng.wait_ge(sem, value)


def tiles_at(l):
    return range(TILES * (l - LEAD) // STEPS, TILES * (l - LEAD + 1) // STEPS)


class Segment:

    def __init__(self, ffn, lstm, base, first=False, last=False, tail=False, has_final=True):
        self.ffn, self.lstm, self.base = ffn, lstm, base
        self.first, self.last, self.tail = first, last, tail
        self.has_final = has_final
        self.steps = range(0 if first else LEAD, STEPS + LEAD)
        self.spare = []
        if first:
            self.spare += [("params", 0), ("xt", 0)]
        for l in self.steps:
            if self.transposes_x(l):
                self.spare.append(("xt", l // GS + 1))
            if l == STEPS and not tail:
                self.spare.append(("stats", 0))
            if l == STEPS + 1 and not tail:
                self.spare.append(("scale", 0))
            if l == LEAD + 1 and has_final:
                self.spare.append(("final", 0))
            if ffn is not None:
                for j in tiles_at(l):
                    if j >= KT and j % KT == 1:
                        self.spare.append(("gate", j // KT - 1))

    def has_step(self, l):
        return not self.tail and not (self.last and l >= STEPS)

    def transposes_x(self, l):
        return not self.tail and l % GS == 0 and not (self.last and l // GS + 1 >= NG)

    def primes(self, l):
        return not self.tail and l % GS == 2 and not (self.last and l // GS + 1 >= NG)

    def use(self, name, k=0):
        return self.base + self.spare.index((name, k))

    def step(self, l):
        return self.lstm * STEPS + l

    def group(self, l):
        return self.lstm * NG + l // GS


def adaln_ffn_kernel(nc, x, cond, Wx, Wh, b, nw, rw, sw1, sb1, sw2, sb2, ew1, eb1, ew2, eb2, out):
    ctx = ExitStack()
    with ctx:
        def sb(name, shape, dt=F32):
            return ctx.enter_context(nc.sbuf_tensor(name, shape, dt))

        def ps(name):
            return ctx.enter_context(nc.psum_tensor(name, [128, 512], F32))

        def sem(name):
            return ctx.enter_context(nc.semaphore(name))

        x_group = [sb(f"x_group{s}", [128, D]) for s in range(2)]
        x_t = sb("x_t", [D, 128])
        x_res = sb("x_res", [128, NG, D])
        out_sb = sb("out_sb", [128, NG, D])
        wx_raw, wh_raw = sb("wx_raw", [D, GATES * D]), sb("wh_raw", [D, GATES * D])
        wx, wh = sb("wx", [D, GATES * D]), sb("wh", [D, GATES * D])
        b_rows = sb("b_rows", [64, D])
        b_scale = sb("b_scale", [64, 1])
        b_scaled = sb("b_scaled", [64, D])
        b_round = sb("b_round", [64, D], F32R)
        b_parts = sb("b_parts", [64, D], F32R)
        gate_mask = sb("gate_mask", [64, GATES, 128])
        gate_maskr = sb("gate_maskr", [64, GATES, 128], F32R)
        gates = [sb(f"gates{s}", [128, GATES + 1, N]) for s in range(2)]
        uv = sb("uv", [128, 2, N])
        tanh_c = sb("tanh_c", [128, N])
        hs = sb("hs", [128, (STEPS + LEAD) * N])
        h_sq = sb("h_sq", [128, TOK])
        params_in = sb("params_in", [ROWS, D])
        params = sb("params", [D, ROWS])
        h_init = sb("h_init", [128, N])
        nw_half = sb("nw_half", [128, 1])
        rw_half = sb("rw_half", [128, E])
        ident, ones = sb("ident", [128, 128]), sb("ones", [128, 1])
        before = sb("before", [128, E, E])
        minus_half = sb("minus_half", [128, NG])
        stats = sb("stats", [128, NG, 1 + E])
        var, rms = sb("var", [128, NG]), sb("rms", [128, NG])
        logits, probs = sb("logits", [128, NG, E]), sb("probs", [128, NG, E])
        above, equal = sb("above", [128, NG, E, E]), sb("equal", [128, NG, E, E])
        rank, chosen = sb("rank", [128, NG, E]), sb("chosen", [128, NG, E])
        total, total_inv = sb("total", [128, NG]), sb("total_inv", [128, NG])
        comb = sb("comb", [128, NG, E])
        comb_bc = [sb(f"comb_bc{s}", [128, TOK]) for s in range(2)]
        xn = sb("xn", [128, TOK])
        xn_hi, xn_lo = sb("xn_hi", [128, TOK], F32R), sb("xn_lo", [128, TOK], F32R)
        w_raw = [sb(f"w_raw{x_}", [128, 2, HID]) for x_ in range(X)]
        w_hi = sb("w_hi", [128, X, 2, HID], F32R)
        w_lo = sb("w_lo", [128, X, 2, HID], F32R)
        h_full = [sb(f"h_full{s}", [128, TOK]) for s in range(RING)]
        h_hi = [sb(f"h_hi{s}", [128, TOK], F32R) for s in range(RING)]
        h_lo = [sb(f"h_lo{s}", [128, TOK], F32R) for s in range(RING)]
        weighted = [sb(f"weighted{s}", [128, TOK]) for s in range(2)]
        acc = sb("acc", [128, TOK])

        gate_ps = [ps(f"gate_ps{s}") for s in range(2)]
        z_ps = [ps(f"z_ps{s}") for s in range(ZB)]
        eo_ps = [ps(f"eo_ps{s}") for s in range(2)]
        spare_ps = ps("spare_ps")

        s_consts = sem("consts")
        s_zeroed = sem("b_rows_zeroed")
        s_const_step = sem("const_step")
        s_params_in = sem("params_in_dma")
        s_wlstm = sem("lstm_weights_dma")
        s_brow = sem("b_rows_dma")
        s_w = [sem(f"w_dma{x_}") for x_ in range(X)]
        s_x = [sem(f"x_group_dma{s}") for s in range(2)]
        s_res = sem("x_res_dma")
        s_out = sem("out_dma")
        s_setup = sem("setup_dve")
        s_wx = sem("wx_scaled")
        s_spare = sem("spare_written")
        s_spare_read = sem("spare_read")
        s_gates = sem("gates_summed")
        s_gates_act = sem("gates_tanh")
        s_uv = sem("uv_done")
        s_c = sem("cell_done")
        s_tanh_c = sem("tanh_c_done")
        s_h = sem("h_done")
        s_w_hi = sem("w_hi_done")
        s_w_split = sem("w_split_done")
        s_z = sem("z_done")
        s_hf = sem("h_full_done")
        s_hi = sem("h_hi_done")
        s_lo = sem("h_lo_done")
        s_l2 = sem("h_used")
        s_wt = sem("weighted_done")
        s_acc = sem("acc_done")
        s_sq = sem("h_sq_done")
        s_var = sem("var_done")
        s_rms = sem("rms_done")
        s_logits = sem("logits_done")
        s_probs = sem("probs_done")
        s_route = sem("route_step")
        s_xhi = sem("xn_hi_done")
        s_xlo = sem("xn_lo_done")
        s_comb = sem("comb_done")
        ROUTE = 9
        SETUP = 6

        block = ctx.enter_context(nc.Block())

        intro = Segment(None, 0, 0, first=True, has_final=False)
        early = Segment(0, 1, len(intro.spare), has_final=False)
        loop_base = early.base + len(early.spare)
        loop_uses = len(Segment(1, 2, 0).spare)
        LOOP_END = CHUNKS - 2

        def looped(i):
            return Segment(i, i + 1, (i - 1) * loop_uses + loop_base)

        late = Segment(CHUNKS - 2, CHUNKS - 1, loop_base + (LOOP_END - 1) * loop_uses, last=True)
        outro = Segment(CHUNKS - 1, None, late.base + len(late.spare), tail=True)
        FINAL_USE = outro.base + len(outro.spare)

        def run(eng, segment):
            segment(intro)
            segment(early)
            with eng.Fori(1, LOOP_END) as i:
                segment(looped(i))
            segment(late)
            segment(outro)

        x_by_group = x.rearrange("n (q t) d -> q t n d", t=GS)
        x_by_chunk = x.rearrange("n (c g t) d -> c t n g d", g=NG, t=GS)
        out_by_chunk = out.rearrange("n (c g t) d -> c t n g d", g=NG, t=GS)

        @block.sync
        def _(sp):
            def load_group(q, slot):
                for t in range(GS):
                    sp.dma_start(x_group[slot][t * N:(t + 1) * N, :], x_by_group[q, t]).then_inc(s_x[slot], 16)

            def load_residual(c):
                for t in range(GS):
                    sp.dma_start(x_res[t * N:(t + 1) * N, :, :], x_by_chunk[c, t]).then_inc(s_res, 16)

            def store(c):
                for t in range(GS):
                    sp.dma_start(out_by_chunk[c, t], out_sb[t * N:(t + 1) * N, :, :]).then_inc(s_out, 16)

            rows = [(ROW_B1, sb1.rearrange("(j p) -> j p", p=128)), (ROW_B1 + KT, eb1.rearrange("e (j p) -> (e j) p", p=128)),
                    (ROW_B2, sb2.rearrange("(a p) -> a p", a=1)), (ROW_B2 + 1, eb2),
                    (ROW_NW, nw.rearrange("(a p) -> a p", a=1)), (ROW_RW, rw), (ROW_H0, cond)]
            for r, src in rows:
                sp.dma_start(params_in[r:r + src.shape[0], :], src).then_inc(s_params_in, 16)
            load_group(0, 0)
            sp.dma_start(wx_raw[:, :], Wx).then_inc(s_wlstm, 16)
            sp.dma_start(wh_raw[:, :], Wh).then_inc(s_wlstm, 16)
            sp.wait_ge(s_zeroed, 1)
            for r in (0, 32):
                sp.dma_start(b_rows[r:r + GATES, :], b.rearrange("(g p) -> g p", p=128)).then_inc(s_brow, 16)
            load_group(1, 1)
            for n in range(X):
                w1, w2 = (sw1, sw2) if n == 0 else (ew1[n - 1], ew2[n - 1])
                sp.dma_start(w_raw[n][:, 0, :], w1).then_inc(s_w[n], 16)
                sp.dma_start(w_raw[n][:, 1, :].rearrange("p (j o) -> p j o", j=KT),
                             w2.rearrange("(j p) o -> p j o", p=128)).then_inc(s_w[n], 16)

            def segment(g):
                if g.first:
                    sp.wait_ge(s_spare, g.use("xt", 0) + 1)
                    load_group(2, 0)
                for l in g.steps:
                    if l == LEAD + 1 and g.ffn is not None:
                        if g.has_final:
                            sp.wait_ge(s_spare_read, g.use("final") + 1)
                            store(g.ffn - 1)
                        load_residual(g.ffn)
                    if g.transposes_x(l) and not g.last:
                        k = l // GS + 1
                        wait(sp, s_spare, g.use("xt", k) + 1)
                        load_group(g.group(l) + 3, k % 2)

            run(sp, segment)
            sp.wait_ge(s_spare_read, FINAL_USE + 1)
            store(CHUNKS - 1)
            sp.wait_ge(s_out, 16 * GS * CHUNKS)

        @block.gpsimd
        def _(pool):
            count = [0]

            def ordered(ins):
                count[0] += 1
                ins.then_inc(s_const_step, 1)
                pool.wait_ge(s_const_step, count[0])

            ordered(nc.gpsimd.memset(ident[:, :], 0.0))
            nc.gpsimd.affine_select(out=ident[:, :], in_=ident[:, :], compare_op=ALU.not_equal, fill=1.0, base=0,
                                    pattern=[[-1, 128]], channel_multiplier=1).then_inc(s_consts, 1)
            nc.gpsimd.memset(b_rows[:, :], 0.0).then_inc(s_zeroed, 1)
            ordered(nc.gpsimd.memset(gate_mask[:, :, :], 0.0))
            ordered(nc.gpsimd.memset(b_scale[:, :], 0.5))
            for r in (0, 32):
                ordered(nc.gpsimd.affine_select(out=gate_mask[:, :, :], in_=gate_mask[:, :, :], compare_op=ALU.not_equal,
                                                fill=1.0, base=-r, pattern=[[-1, GATES], [0, 128]], channel_multiplier=1))
                ordered(nc.gpsimd.affine_select(out=b_scale[:, :], in_=b_scale[:, :], compare_op=ALU.not_equal,
                                                fill=1.0, base=-(r + GATES - 1), pattern=[[0, 1]], channel_multiplier=1))
            ordered(nc.gpsimd.memset(gates[0][:, GATES, :], 0.0))
            nc.gpsimd.memset(ones[:, :], 1.0).then_inc(s_consts, 1)
            ordered(nc.gpsimd.memset(before[:, :, :], 1.0))
            ordered(nc.gpsimd.affine_select(out=before[:, :, :], in_=before[:, :, :], compare_op=ALU.is_gt,
                                            fill=0.0, base=0, pattern=[[1, E], [-1, E]], channel_multiplier=0))
            nc.gpsimd.memset(minus_half[:, :], -0.5).then_inc(s_consts, 1)
            pool.wait_ge(s_consts, 3)

            def squares(g, k):
                pool.wait_ge(s_h, g.step(GS * k + GS))
                cols = slice(k * 128, (k + 1) * 128)
                nc.gpsimd.tensor_tensor(h_sq[:, cols], hs[:, cols], hs[:, cols], ALU.mult).then_inc(s_sq, 1)

            def segment(g):
                for l in g.steps:
                    if not g.tail and l % GS == GS - 1 and l < STEPS:
                        squares(g, l // GS)
                    if g.ffn is not None:
                        for j in tiles_at(l):
                            n = j // KT
                            if j % KT == KT - 1 and n > 0:
                                pool.wait_ge(s_wt, g.ffn * X + n + 1)
                                wait(pool, s_acc, g.ffn * E + n - 1)
                                nc.gpsimd.tensor_tensor(acc[:, :], acc[:, :], weighted[n % 2][:, :], ALU.add).then_inc(s_acc, 1)
                    if not g.tail and l == STEPS:
                        pool.wait_ge(s_var, g.lstm + 1)
                        nc.gpsimd.tensor_tensor(rms[:, :], var[:, :], minus_half[:, :], ALU.pow).then_inc(s_rms, 1)
                        pool.wait_ge(s_rms, g.lstm + 1)
                        nc.gpsimd.tensor_tensor(logits[:, :, :], stats[:, :, 1:1 + E],
                                                rms[:, :].unsqueeze(2).broadcast_to([128, NG, E]), ALU.mult).then_inc(s_logits, 1)

            run(pool, segment)

        @block.scalar
        def _(act):
            act.wait_ge(s_wlstm, 32)
            S = (GATES - 1) * D
            nc.scalar.mul(wx[:, 0:S], wx_raw[:, 0:S], 0.5)
            nc.scalar.mul(wx[:, S:], wx_raw[:, S:], 1.0)
            nc.scalar.mul(wh[:, 0:S], wh_raw[:, 0:S], 0.25)
            nc.scalar.mul(wh[:, S:], wh_raw[:, S:], 0.5).then_inc(s_wx, 1)

            def relu(g, j):
                J = g.ffn * TILES + j
                act.wait_ge(s_z, J + 1)
                wait(act, s_l2, J - RING + 1)
                bias = params[:, ROW_B1 + j:ROW_B1 + j + 1]
                if j % 2 == 0:
                    nc.scalar.activation(h_hi[j % RING][:, :], z_ps[j % ZB][:, :], ACT.Relu, bias=bias)
                nc.scalar.activation(h_full[j % RING][:, :], z_ps[j % ZB][:, :], ACT.Relu, bias=bias).then_inc(s_hf, 1)

            def segment(g):
                for l in g.steps:
                    if g.has_step(l):
                        s = g.step(l)
                        act.wait_ge(s_gates, s + 1)
                        nc.scalar.activation(gates[l % 2][:, 0:GATES, :],
                                             gate_ps[(l // GS) % 2][:, :].rearrange("p (g t n) -> p g t n", g=GATES, n=N)[:, :, l % GS, :],
                                             ACT.Tanh).then_inc(s_gates_act, 1)
                        act.wait_ge(s_c, s + 1)
                        nc.scalar.activation(tanh_c[:, :], gates[(l + 1) % 2][:, GATES, :], ACT.Tanh, scale=0.5).then_inc(s_tanh_c, 1)
                    if g.first:
                        n, w = l // 2, l % 2
                        act.wait_ge(s_w[n], 32)
                        nc.scalar.copy(w_hi[:, n, w, :], w_raw[n][:, w, :]).then_inc(s_w_hi, 1)
                    if g.ffn is not None:
                        if l == LEAD:
                            for j in range(LAG):
                                relu(g, j)
                        for j in tiles_at(l):
                            if j + LAG < TILES:
                                relu(g, j + LAG)
                            if j >= KT and j % KT == 1:
                                e = j // KT - 1
                                act.wait_ge(s_spare, g.use("gate", e) + 1)
                                wait(act, s_wt, g.ffn * X + e)
                                nc.scalar.copy(comb_bc[e % 2][:, :], spare_ps[:, :]).then_inc(s_spare_read, 1)
                    if not g.tail and l == STEPS:
                        act.wait_ge(s_logits, g.lstm + 1)
                        nc.scalar.activation(probs[:, :, :], logits[:, :, :], ACT.Sigmoid).then_inc(s_probs, 1)

            run(act, segment)

        @block.vector
        def _(dve):
            setup = [0]

            def ordered(ins):
                setup[0] += 1
                ins.then_inc(s_setup, 1)
                dve.wait_ge(s_setup, setup[0])

            dve.wait_ge(s_spare, intro.use("params") + 1)
            ordered(nc.vector.tensor_copy(params[:, :], spare_ps[:, 0:ROWS]))
            nc.vector.tensor_scalar(h_init[:, :], params[:, ROW_H0:ROW_H0 + N], 2.0, None, ALU.mult).then_inc(s_spare_read, 1)
            ordered(nc.vector.tensor_scalar(nw_half[:, :], params[:, ROW_NW:ROW_NW + 1], 0.5, None, ALU.mult))
            dve.wait_ge(s_spare, intro.use("xt", 0) + 1)
            nc.vector.tensor_copy(x_t[:, :], spare_ps[:, 0:128]).then_inc(s_spare_read, 1)
            dve.wait_ge(s_brow, 32)
            dve.wait_ge(s_consts, 3)
            ordered(nc.vector.tensor_scalar(b_scaled[:, :], b_rows[:, :], b_scale[:, 0:1], None, ALU.mult))
            ordered(nc.vector.tensor_copy(b_round[:, :], b_scaled[:, :]))
            nc.vector.tensor_copy(gate_maskr[:, :, :], gate_mask[:, :, :])
            nc.vector.tensor_copy(b_parts[0:32, :], b_scaled[0:32, :])
            ordered(nc.vector.tensor_tensor(b_parts[32:64, :], b_scaled[32:64, :], b_round[32:64, :].bitcast(F32), ALU.subtract))
            ordered(nc.vector.tensor_scalar(rw_half[:, :], params[:, ROW_RW:ROW_RW + E], nw_half[:, 0:1], None, ALU.mult))
            assert setup[0] == SETUP

            def split_odd(g, j):
                J = g.ffn * TILES + j
                dve.wait_ge(s_hf, J + 1)
                if j % 2:
                    nc.vector.tensor_copy(h_hi[j % RING][:, :], h_full[j % RING][:, :]).then_inc(s_hi, 1)
                    dve.wait_ge(s_hi, g.ffn * (TILES // 2) + j // 2 + 1)
                nc.vector.tensor_tensor(h_lo[j % RING][:, :], h_full[j % RING][:, :],
                                        h_hi[j % RING][:, :].bitcast(F32), ALU.subtract).then_inc(s_lo, 1)

            def weigh(g, n):
                dve.wait_ge(s_l2, g.ffn * TILES + (n + 1) * KT)
                b2 = params[:, ROW_B2 + n:ROW_B2 + n + 1]
                if n == 0:
                    nc.vector.tensor_scalar(acc[:, :], eo_ps[0][:, :], b2, None, ALU.add).then_inc(s_wt, 1)
                else:
                    wait(dve, s_spare_read, g.use("gate", n - 1) + 1)
                    wait(dve, s_acc, g.ffn * E + n - 2)
                    nc.vector.scalar_tensor_tensor(weighted[n % 2][:, :], eo_ps[n % 2][:, :], b2, comb_bc[(n - 1) % 2][:, :],
                                                   ALU.add, ALU.mult).then_inc(s_wt, 1)

            def final(ffn, use):
                dve.wait_ge(s_spare, use + 1)
                dve.wait_ge(s_res, 16 * GS * (ffn + 1))
                wait(dve, s_out, 16 * GS * ffn)
                nc.vector.tensor_tensor(out_sb[:, :, :], spare_ps[:, :].rearrange("p (g d) -> p g d", g=NG),
                                        x_res[:, :, :], ALU.add).then_inc(s_spare_read, 1)

            def split_xn(g):
                c = g.lstm
                wait(dve, s_z, c * TILES)
                nc.vector.tensor_copy(xn_hi[:, :], xn[:, :]).then_inc(s_xhi, 1)
                dve.wait_ge(s_xhi, c + 1)
                nc.vector.tensor_tensor(xn_lo[:, :], xn[:, :], xn_hi[:, :].bitcast(F32), ALU.subtract).then_inc(s_xlo, 1)

            def route(g):
                c, n = g.lstm, [0]

                def ordered(ins):
                    n[0] += 1
                    ins.then_inc(s_route, 1)
                    dve.wait_ge(s_route, c * ROUTE + n[0])

                dve.wait_ge(s_probs, c + 1)
                other = probs[:, :, :].unsqueeze(2).broadcast_to([128, NG, E, E])
                own = probs[:, :, :].unsqueeze(3).broadcast_to([128, NG, E, E])
                nc.vector.tensor_tensor(above[:, :, :, :], other, own, ALU.is_gt).then_inc(s_route, 1)
                n[0] += 1
                ordered(nc.vector.tensor_tensor(equal[:, :, :, :], other, own, ALU.is_equal))
                ordered(nc.vector.tensor_tensor(equal[:, :, :, :], equal[:, :, :, :],
                                                before[:, :, :].unsqueeze(1).broadcast_to([128, NG, E, E]), ALU.mult))
                ordered(nc.vector.tensor_tensor(above[:, :, :, :], above[:, :, :, :], equal[:, :, :, :], ALU.add))
                ordered(nc.vector.tensor_reduce(rank[:, :, :], above[:, :, :, :], AX.X, ALU.add))
                ordered(nc.vector.scalar_tensor_tensor(chosen[:, :, :], rank[:, :, :], 1.5, probs[:, :, :], ALU.is_lt, ALU.mult))
                ordered(nc.vector.tensor_reduce(total[:, :], chosen[:, :, :], AX.X, ALU.add))
                ordered(nc.vector.tensor_scalar(total_inv[:, :], total[:, :], EPS_TOP, None, ALU.add))
                ordered(nc.vector.reciprocal(total[:, :], total_inv[:, :]))
                nc.vector.tensor_tensor(comb[:, :, :], chosen[:, :, :], total[:, :].unsqueeze(2).broadcast_to([128, NG, E]),
                                        ALU.mult).then_inc(s_comb, 1)
                assert n[0] == ROUTE

            def segment(g):
                for l in g.steps:
                    if g.has_step(l):
                        s, now, nxt = g.step(l), gates[l % 2], gates[(l + 1) % 2]
                        dve.wait_ge(s_gates_act, s + 1)
                        wait(dve, s_c, s)
                        nc.vector.scalar_tensor_tensor(uv[:, :, :], now[:, 0:2, :], 1.0, now[:, 3:5, :], ALU.add, ALU.mult).then_inc(s_uv, 1)
                        dve.wait_ge(s_uv, s + 1)
                        nc.vector.scalar_tensor_tensor(nxt[:, GATES, :], uv[:, 1, :], 0.5, uv[:, 0, :], ALU.mult, ALU.add).then_inc(s_c, 1)
                        dve.wait_ge(s_tanh_c, s + 1)
                        nc.vector.scalar_tensor_tensor(hs[:, l * N:(l + 1) * N], now[:, 2, :], 1.0, tanh_c[:, :], ALU.add, ALU.mult).then_inc(s_h, 1)
                    if g.transposes_x(l):
                        wait(dve, s_spare, g.use("xt", l // GS + 1) + 1)
                        nc.vector.tensor_copy(x_t[:, :], spare_ps[:, 0:128]).then_inc(s_spare_read, 1)
                    if not g.tail and l == STEPS:
                        dve.wait_ge(s_spare, g.use("stats") + 1)
                        nc.vector.tensor_copy(stats[:, :, :], spare_ps[:, 0:NG * (1 + E)].rearrange("p (g k) -> p g k", g=NG)).then_inc(s_spare_read, 1)
                        dve.wait_ge(s_spare_read, g.use("stats") + 1)
                        nc.vector.tensor_scalar(var[:, :], stats[:, :, 0], 1.0 / (4 * D), EPS_RMS, ALU.mult, ALU.add).then_inc(s_var, 1)
                    if not g.tail and l == STEPS + 1:
                        dve.wait_ge(s_spare, g.use("scale") + 1)
                        nc.vector.scalar_tensor_tensor(xn[:, :], hs[:, 0:TOK], nw_half[:, 0:1], spare_ps[:, :], ALU.mult, ALU.mult).then_inc(s_spare_read, 1)
                        dve.wait_ge(s_spare_read, g.use("scale") + 1)
                        if g.has_step(l):
                            nc.vector.tensor_copy(hs[:, 0:LEAD * N], hs[:, TOK:TOK + LEAD * N])
                    if l == LEAD + 1 and g.has_final:
                        final(g.ffn - 1, g.use("final"))
                    if g.first:
                        n, w = l // 2, l % 2
                        dve.wait_ge(s_w_hi, l + 1)
                        nc.vector.tensor_tensor(w_lo[:, n, w, :], w_raw[n][:, w, :], w_hi[:, n, w, :].bitcast(F32), ALU.subtract).then_inc(s_w_split, 1)
                    if g.ffn is not None:
                        if l == LEAD:
                            for j in range(LAG):
                                split_odd(g, j)
                        for j in tiles_at(l):
                            if j + LAG < TILES:
                                split_odd(g, j + LAG)
                            if j % KT == KT - 1 and j < TILES - 1:
                                weigh(g, j // KT)
                    if not g.tail and l == STEPS + 1:
                        split_xn(g)
                    if g.ffn is not None and l == STEPS + LEAD - 1:
                        weigh(g, X - 1)
                    if not g.tail and l == STEPS + 1:
                        route(g)

            run(dve, segment)
            final(CHUNKS - 1, FINAL_USE)

        @block.tensor
        def _(pe):
            def to_spare(g_use):
                wait(pe, s_spare_read, g_use)

            def transpose_x(q_slot, q_use, waits):
                pe.wait_ge(s_x[q_slot], waits)
                to_spare(q_use)
                nc.tensor.transpose(spare_ps[:, 0:128], x_group[q_slot][:, :], ident[:, :]).then_inc(s_spare, 1)

            def prime(q_bank):
                bank = gate_ps[q_bank]
                nc.tensor.matmul(bank[:, :], b_parts[:, :], gate_maskr[:, :, :].rearrange("p g c -> p (g c)"), start=True, stop=False,
                                 skip_group_check=True)
                for k in range(GATES):
                    nc.tensor.matmul(bank[:, k * 128:(k + 1) * 128], wx[:, k * D:(k + 1) * D], x_t[:, :], start=False, stop=False,
                                     skip_group_check=True)

            def lstm_step(g, l):
                s = g.step(l)
                if g.first and l == 0:
                    h = h_init[:, :]
                else:
                    wait(pe, s_h, s)
                    prev = l - 1 if (l > LEAD or g.first) else STEPS + LEAD - 1
                    h = hs[:, prev * N:(prev + 1) * N]
                bank = gate_ps[(l // GS) % 2]
                for k in range(GATES):
                    c0 = k * 128 + (l % GS) * N
                    last = nc.tensor.matmul(bank[:, c0:c0 + N], wh[:, k * D:(k + 1) * D], h, start=False, stop=(l % GS == GS - 1),
                                            skip_group_check=True)
                last.then_inc(s_gates, 1)

            def layer1(g, j):
                J = g.ffn * TILES + j
                n, k = j // KT, j % KT
                if j == 0:
                    pe.wait_ge(s_xlo, g.ffn + 1)
                wait(pe, s_hf, J - ZB + 1)
                if isinstance(g.ffn, int) and g.ffn == 0 and k == 0:
                    pe.wait_ge(s_w_split, 2 * n + 1)
                z, cols = z_ps[j % ZB][:, :], slice(k * 128, (k + 1) * 128)
                nc.tensor.matmul(z, w_hi[:, n, 0, cols], xn_hi[:, :], start=True, stop=False)
                nc.tensor.matmul(z, w_lo[:, n, 0, cols], xn_hi[:, :], start=False, stop=False)
                nc.tensor.matmul(z, w_hi[:, n, 0, cols], xn_lo[:, :], start=False, stop=True).then_inc(s_z, 1)

            def layer2(g, j):
                J = g.ffn * TILES + j
                n, k = j // KT, j % KT
                pe.wait_ge(s_lo, J + 1)
                if k == 0:
                    wait(pe, s_wt, g.ffn * X + (n - 1 if n else 0))
                if isinstance(g.ffn, int) and g.ffn == 0 and k == 0:
                    pe.wait_ge(s_w_split, 2 * n + 2)
                eo, cols = eo_ps[n % 2][:, :], slice(k * 128, (k + 1) * 128)
                nc.tensor.matmul(eo, w_hi[:, n, 1, cols], h_hi[j % RING][:, :], start=(k == 0), stop=False)
                nc.tensor.matmul(eo, w_lo[:, n, 1, cols], h_hi[j % RING][:, :], start=False, stop=False)
                nc.tensor.matmul(eo, w_hi[:, n, 1, cols], h_lo[j % RING][:, :], start=False, stop=(k == KT - 1)).then_inc(s_l2, 1)

            def broadcast_columns(src):
                for k in range(NG):
                    last = nc.tensor.transpose(spare_ps[:, k * 128:(k + 1) * 128], src(k).broadcast_to([128, 128]), ident[:, :])
                last.then_inc(s_spare, 1)

            def final(ffn, use):
                pe.wait_ge(s_acc, E * (ffn + 1))
                to_spare(use)
                for k in range(NG):
                    last = nc.tensor.transpose(spare_ps[:, k * 128:(k + 1) * 128], acc[:, k * 128:(k + 1) * 128], ident[:, :])
                last.then_inc(s_spare, 1)

            def segment(g):
                if g.first:
                    pe.wait_ge(s_consts, 3)
                    pe.wait_ge(s_params_in, 7 * 16)
                    nc.tensor.transpose(spare_ps[:, 0:ROWS], params_in[:, :], ident[0:ROWS, 0:ROWS]).then_inc(s_spare, 1)
                    transpose_x(0, g.use("xt", 0), 16 * GS)
                    pe.wait_ge(s_setup, SETUP)
                    pe.wait_ge(s_wx, 1)
                    wait(pe, s_spare_read, g.use("xt", 0) + 1)
                    prime(0)
                for l in g.steps:
                    k = l // GS + 1
                    if g.has_step(l):
                        lstm_step(g, l)
                    if g.transposes_x(l):
                        transpose_x(k % 2, g.use("xt", k), (g.lstm * (NG // 2) + k // 2 + 1) * (16 * GS))
                    if g.primes(l):
                        if g.first or l > LEAD:
                            wait(pe, s_spare_read, g.use("xt", k) + 1)
                        prime(k % 2)
                    if not g.tail and l == STEPS:
                        pe.wait_ge(s_sq, NG * (g.lstm + 1))
                        to_spare(g.use("stats"))
                        for q in range(NG):
                            cols, c0 = slice(q * 128, (q + 1) * 128), q * (1 + E)
                            nc.tensor.matmul(spare_ps[:, c0:c0 + 1], h_sq[:, cols], ones[:, :], start=True, stop=True)
                            last = nc.tensor.matmul(spare_ps[:, c0 + 1:c0 + 1 + E], hs[:, cols], rw_half[:, :], start=True, stop=True)
                        last.then_inc(s_spare, 1)
                    if not g.tail and l == STEPS + 1:
                        pe.wait_ge(s_rms, g.lstm + 1)
                        to_spare(g.use("scale"))
                        broadcast_columns(lambda k: rms[:, k:k + 1])
                    if l == LEAD + 1 and g.has_final:
                        final(g.ffn - 1, g.use("final"))
                    if g.ffn is not None:
                        if l == LEAD:
                            for j in range(LAG):
                                layer1(g, j)
                        for j in tiles_at(l):
                            if j + LAG < TILES:
                                layer1(g, j + LAG)
                            layer2(g, j)
                            if j >= KT and j % KT == 1:
                                e = j // KT - 1
                                if e == 0:
                                    pe.wait_ge(s_comb, g.ffn + 1)
                                to_spare(g.use("gate", e))
                                broadcast_columns(lambda k: comb[:, k, e:e + 1])

            run(pe, segment)
            final(CHUNKS - 1, FINAL_USE)


_INS = ['x', 'cond_1024', 'L0_cond_Wx', 'L0_cond_Wh', 'L0_cond_b', 'L0_ffn_norm_weight', 'L0_ffn_router_w', 'L0_ffn_sw1',
        'L0_ffn_sb1', 'L0_ffn_sw2', 'L0_ffn_sb2', 'L0_ffn_ew1', 'L0_ffn_eb1', 'L0_ffn_ew2', 'L0_ffn_eb2']
_OUTS = [((N, T, D), 'float32')]


def kernel(**inputs):
    import numpy as _np
    import concourse.bacc as _bacc
    from concourse import mybir as _mybir
    from concourse.bass_utils import run_bass_kernel_spmd as _run

    nc = _bacc.Bacc("TRN2", target_bir_lowering=False, num_devices=1)
    arrays, args = {}, []
    for name in _INS:
        a = _np.ascontiguousarray(inputs[name])
        arrays[f"in_{name}_dram"] = a
        args.append(nc.dram_tensor(f"in_{name}_dram", a.shape, _mybir.dt.from_np(a.dtype), kind="ExternalInput").ap())
    for i, (shape, dtype) in enumerate(_OUTS):
        dt = _mybir.dt.from_np(_np.dtype(dtype))
        args.append(nc.dram_tensor(f"out_{i}_dram", shape, dt, kind="ExternalOutput").ap())
    adaln_ffn_kernel(nc, *args)
    r = _run(nc, [arrays], core_ids=[0])
    return r.results[0]["out_0_dram"]
```

```python
import concourse.bass as bass
from concourse import mybir
from contextlib import ExitStack

F32 = mybir.dt.float32
F32R = mybir.dt.float32r
BF16 = mybir.dt.bfloat16
F16 = mybir.dt.float16
ALU = mybir.AluOpType
ACT = mybir.ActivationFunctionType
AX = mybir.AxisListType

N = 32
T = 128
D = 128
HID = 512
E = 8
X = E + 1
KT = HID // 128
GATES = 4
GS = 128 // N
STEPS = 16
TOK = STEPS * N
NG = STEPS // GS
CHUNKS = T // STEPS
TILES = X * KT
LEAD = 4
LAG = 3
ZB = 3
WRING = 5
RING = 6
H_SCALE = 2.0 ** 12
EPS_RMS = 1e-8
EPS_TOP = 1e-6

ROW_B1 = 0
ROW_B2 = ROW_B1 + TILES
ROW_NW = ROW_B2 + X
ROW_RW = ROW_NW + 1
ROW_H0 = ROW_RW + E
ROWS = ROW_H0 + N


def wait(eng, sem, value):
    if not isinstance(value, int) or value > 0:
        eng.wait_ge(sem, value)


class Segment:

    def __init__(self, ffn, lstm, base, start=LEAD, lead=LEAD, last=False, has_final=True):
        self.ffn, self.lstm, self.base = ffn, lstm, base
        self.first, self.last, self.tail = ffn is None, last, lstm is None
        self.has_final = has_final
        self.start, self.end = start, STEPS + lead
        self.before = STEPS + start
        self.steps = range(start, self.end)
        self.stats_at, self.scale_at = (None, None) if self.tail else (self.end - lead // 2 - 1, self.end - lead // 2)
        self.spare = []
        if self.first:
            self.spare += [("params", 0), ("xt", 0)]
        for l in self.steps:
            if self.transposes_x(l):
                self.spare.append(("xt", l // GS + 1))
            if l == self.stats_at:
                self.spare.append(("stats", 0))
            if l == self.scale_at:
                self.spare.append(("scale", 0))
            if l == start + 1 and has_final:
                self.spare.append(("final", 0))
            if l == start + 1 and ffn is not None:
                self.spare.append(("comb", 0))

    def tiles_at(self, l):
        if self.ffn is None or l < self.start:
            return range(0)
        n = self.end - self.start
        return range(TILES * (l - self.start) // n, TILES * (l - self.start + 1) // n)

    def first_layer(self, l):
        return list(range(LAG if l == self.start and self.ffn is not None else 0)) + [
            j + LAG for j in self.tiles_at(l) if j + LAG < TILES]

    def held_back(self, l):
        return [j for j in self.first_layer(l)[-1:] if j < TILES - 1]

    def taken_on(self, l):
        return [j for j in self.first_layer(l) if j not in self.held_back(l)]

    def weighed_at(self, l):
        return [j // KT - 1 for j in self.tiles_at(l) if j >= KT and j % KT == 1] + [X - 1] * (
            l == self.end - 1 and self.ffn is not None)

    def has_step(self, l):
        return not self.tail and not (self.last and l >= STEPS)

    def transposes_x(self, l):
        return not self.tail and l % GS == 0 and not (self.last and l // GS + 1 >= NG)

    def primes(self, l):
        return not self.tail and l % GS == 2 and not (self.last and l // GS + 1 >= NG)

    def use(self, name, k=0):
        return self.base + self.spare.index((name, k))

    def step(self, l):
        return self.lstm * STEPS + l

    def group(self, l):
        return self.lstm * NG + l // GS


def adaln_ffn_kernel(nc, x, cond, Wx, Wh, b, nw, rw, sw1, sb1, sw2, sb2, ew1, eb1, ew2, eb2, out):
    ctx = ExitStack()
    with ctx:
        def sb(name, shape, dt=F32):
            return ctx.enter_context(nc.sbuf_tensor(name, shape, dt))

        def ps(name):
            return ctx.enter_context(nc.psum_tensor(name, [128, 512], F32))

        def sem(name):
            return ctx.enter_context(nc.semaphore(name))

        x_group = [sb(f"x_group{s}", [128, D]) for s in range(2)]
        x_t = sb("x_t", [D, 128])
        x_res = sb("x_res", [128, NG, D])
        out_sb = sb("out_sb", [128, NG, D])
        wx_raw, wh_raw = sb("wx_raw", [D, GATES * D]), sb("wh_raw", [D, GATES * D])
        wx, wh = sb("wx", [D, GATES * D]), sb("wh", [D, GATES * D])
        wh_parts = sb("wh_parts", [D, 3, GATES * D], BF16)
        wh_rest = sb("wh_rest", [D, 2, GATES * D])
        b_rows = sb("b_rows", [64, D])
        b_scale = sb("b_scale", [64, 1])
        b_scaled = sb("b_scaled", [64, D])
        b_round = sb("b_round", [64, D], F32R)
        b_parts = sb("b_parts", [64, D], F32R)
        gate_mask = sb("gate_mask", [64, GATES, 128])
        gate_maskr = sb("gate_maskr", [64, GATES, 128], F32R)
        gates = [sb(f"gates{s}", [128, GATES + 1, N]) for s in range(2)]
        uv = sb("uv", [128, 2, N])
        tanh_c = sb("tanh_c", [128, N])
        o_scaled = sb("o_scaled", [128, N])
        hs = sb("hs", [128, (STEPS + LEAD) * N])
        h_a, h_b = sb("h_a", [128, (STEPS + LEAD) * N], F16), sb("h_b", [128, (STEPS + LEAD) * N], F16)
        rw_parts = sb("rw_parts", [128, 3, E], BF16)
        rw_rest = sb("rw_rest", [128, 2, E])
        h_sq = sb("h_sq", [128, TOK])
        params_in = sb("params_in", [ROWS, D])
        params = sb("params", [D, ROWS])
        h_init = sb("h_init", [128, N])
        nw_scaled = sb("nw_scaled", [128, 1])
        rw_scaled = sb("rw_scaled", [128, E])
        ident, ones = sb("ident", [128, 128]), sb("ones", [128, 1])
        before = sb("before", [128, E, E])
        minus_half = sb("minus_half", [128, NG])
        stats = sb("stats", [128, NG, 1 + 3 * E])
        raw_logits = sb("raw_logits", [128, NG, E])
        var, rms = sb("var", [128, NG]), sb("rms", [128, NG])
        logits, probs = sb("logits", [128, NG, E]), sb("probs", [128, NG, E])
        above, equal = sb("above", [128, NG, E, E]), sb("equal", [128, NG, E, E])
        rank, chosen = sb("rank", [128, NG, E]), sb("chosen", [128, NG, E])
        total, total_inv = sb("total", [128, NG]), sb("total_inv", [128, NG])
        comb = sb("comb", [128, E, NG])
        comb_rows = sb("comb_rows", [E * NG, 128])
        comb_bc = sb("comb_bc", [128, E, TOK])
        xn = sb("xn", [128, TOK])
        xn_hi, xn_lo = sb("xn_hi", [128, TOK], F32R), sb("xn_lo", [128, TOK], F32R)
        w_raw = [sb(f"w_raw{x_}", [128, 2, HID]) for x_ in range(WRING)]
        w_hi = sb("w_hi", [128, X, 2, HID], F32R)
        w_lo = sb("w_lo", [128, X, 2, HID], F32R)
        h_full = [sb(f"h_full{s}", [128, TOK]) for s in range(RING)]
        h_hi = [sb(f"h_hi{s}", [128, TOK], F32R) for s in range(RING)]
        h_lo = [sb(f"h_lo{s}", [128, TOK], F32R) for s in range(RING)]
        weighted = [sb(f"weighted{s}", [128, TOK]) for s in range(2)]
        acc = sb("acc", [128, TOK])

        gate_ps = [ps(f"gate_ps{s}") for s in range(2)]
        z_ps = [ps(f"z_ps{s}") for s in range(ZB)]
        eo_ps = [ps(f"eo_ps{s}") for s in range(2)]
        spare_ps = ps("spare_ps")

        s_consts = sem("consts")
        s_zeroed = sem("b_rows_zeroed")
        s_const_step = sem("const_step")
        s_params_in = sem("params_in_dma")
        s_wlstm = sem("lstm_weights_dma")
        s_brow = sem("b_rows_dma")
        s_w = [sem(f"w_dma{x_}") for x_ in range(X)]
        s_x = [sem(f"x_group_dma{s}") for s in range(2)]
        s_res = sem("x_res_dma")
        s_out = sem("out_dma")
        s_setup = sem("setup_dve")
        s_wx = sem("wx_scaled")
        s_spare = sem("spare_written")
        s_spare_read = sem("spare_read")
        s_gates = sem("gates_summed")
        s_gates_act = sem("gates_tanh")
        s_uv = sem("uv_done")
        s_c = sem("cell_done")
        s_tanh_c = sem("tanh_c_done")
        s_o = sem("o_scaled_done")
        s_ha = sem("h_a_done")
        s_hs = sem("hs_done")
        s_wh = sem("wh_split")
        s_h = sem("h_done")
        s_w_hi = sem("w_hi_done")
        s_w_split = sem("w_split_done")
        s_z = sem("z_done")
        s_hf = sem("h_full_done")
        s_hi = sem("h_hi_done")
        s_lo = sem("h_lo_done")
        s_l2 = sem("h_used")
        s_wt = sem("weighted_done")
        s_acc = sem("acc_done")
        s_sq = sem("h_sq_done")
        s_copied = sem("lead_copied")
        s_raw = sem("raw_logits_done")
        s_var = sem("var_done")
        s_rms = sem("rms_done")
        s_logits = sem("logits_done")
        s_probs = sem("probs_done")
        s_route = sem("route_step")
        s_xhi = sem("xn_hi_done")
        s_xlo = sem("xn_lo_done")
        s_comb = sem("comb_done")
        s_masked = sem("ties_masked")
        s_row = sem("comb_rows_dma")
        s_bc = [sem(f"comb_bc_dma{s}") for s in range(2)]
        ROUTE = 7
        SETUP = 6
        SPLIT3 = 5

        block = ctx.enter_context(nc.Block())

        FIRST_LEAD = 2
        intro = Segment(None, 0, 0, start=0, lead=FIRST_LEAD, has_final=False)
        early = Segment(0, 1, len(intro.spare), start=FIRST_LEAD, has_final=False)
        loop_base = early.base + len(early.spare)
        loop_uses = len(Segment(1, 2, 0).spare)
        LOOP_END = CHUNKS - 2

        def looped(i):
            return Segment(i, i + 1, (i - 1) * loop_uses + loop_base)

        late = Segment(CHUNKS - 2, CHUNKS - 1, loop_base + (LOOP_END - 1) * loop_uses, last=True)
        outro = Segment(CHUNKS - 1, None, late.base + len(late.spare))
        FINAL_USE = outro.base + len(outro.spare)

        def run(eng, segment):
            segment(intro)
            segment(early)
            with eng.Fori(1, LOOP_END) as i:
                segment(looped(i))
            segment(late)
            segment(outro)

        comb_dram = nc.dram_tensor("comb_scratch", (CHUNKS, E * TOK), F32, kind="Internal").ap()

        x_by_group = x.rearrange("n (q t) d -> q t n d", t=GS)
        x_by_chunk = x.rearrange("n (c g t) d -> c t n g d", g=NG, t=GS)
        out_by_chunk = out.rearrange("n (c g t) d -> c t n g d", g=NG, t=GS)

        @block.sync
        def _(sp):
            def load_group(q, slot):
                for t in range(GS):
                    sp.dma_start(x_group[slot][t * N:(t + 1) * N, :], x_by_group[q, t]).then_inc(s_x[slot], 16)

            def load_residual(c):
                for t in range(GS):
                    sp.dma_start(x_res[t * N:(t + 1) * N, :, :], x_by_chunk[c, t]).then_inc(s_res, 16)

            def store(c):
                for t in range(GS):
                    sp.dma_start(out_by_chunk[c, t], out_sb[t * N:(t + 1) * N, :, :]).then_inc(s_out, 16)

            rows = [(ROW_B1, sb1.rearrange("(j p) -> j p", p=128)), (ROW_B1 + KT, eb1.rearrange("e (j p) -> (e j) p", p=128)),
                    (ROW_B2, sb2.rearrange("(a p) -> a p", a=1)), (ROW_B2 + 1, eb2),
                    (ROW_NW, nw.rearrange("(a p) -> a p", a=1)), (ROW_RW, rw), (ROW_H0, cond)]
            load_group(0, 0)
            for r, src in rows:
                sp.dma_start(params_in[r:r + src.shape[0], :], src).then_inc(s_params_in, 16)
            load_group(1, 1)

            def load_expert(n):
                w1, w2 = (sw1, sw2) if n == 0 else (ew1[n - 1], ew2[n - 1])
                sp.dma_start(w_raw[n % WRING][:, 0, :], w1).then_inc(s_w[n], 16)
                sp.dma_start(w_raw[n % WRING][:, 1, :].rearrange("p (j o) -> p j o", j=KT),
                             w2.rearrange("(j p) o -> p j o", p=128)).then_inc(s_w[n], 16)

            for n in range(WRING):
                load_expert(n)

            def segment(g):
                if g.first:
                    sp.wait_ge(s_spare, g.use("xt", 0) + 1)
                    load_group(2, 0)
                for l in g.steps:
                    if l == g.start + 1 and g.ffn is not None:
                        if g.has_final:
                            sp.wait_ge(s_spare_read, g.use("final") + 1)
                            store(g.ffn - 1)
                        load_residual(g.ffn)
                        sp.wait_ge(s_spare_read, g.use("comb") + 1)
                        sp.dma_start(comb_dram[g.ffn].rearrange("(r t) -> r t", t=128), comb_rows[:, :]).then_inc(s_row, 16)
                        sp.wait_ge(s_row, (g.ffn + 1) * 16)
                        for half in range(2):
                            wait(sp, s_wt, g.ffn * X - (0 if half else E // 2))
                            sp.dma_start(comb_bc[:, half * E // 2:(half + 1) * E // 2, :].rearrange("p e t -> p (e t)"),
                                         comb_dram[g.ffn, half * E // 2 * TOK:(half + 1) * E // 2 * TOK].partition_broadcast(128)
                                         ).then_inc(s_bc[half], 16)
                    n = WRING + l // 2 - 1
                    if g.first and l % 2 == 0 and WRING <= n < X:
                        sp.wait_ge(s_w_split, 2 * (n - WRING + 1))
                        load_expert(n)
                    if g.transposes_x(l) and not g.last:
                        k = l // GS + 1
                        wait(sp, s_spare, g.use("xt", k) + 1)
                        load_group(g.group(l) + 3, k % 2)

            run(sp, segment)
            sp.wait_ge(s_spare_read, FINAL_USE + 1)
            store(CHUNKS - 1)
            sp.wait_ge(s_out, 16 * GS * CHUNKS)

        @block.gpsimd
        def _(pool):
            count = [0]

            def ordered(ins):
                count[0] += 1
                ins.then_inc(s_const_step, 1)
                pool.wait_ge(s_const_step, count[0])

            nc.gpsimd.memset(b_rows[:, :], 0.0).then_inc(s_zeroed, 1)
            ordered(nc.gpsimd.memset(ident[:, :], 0.0))
            nc.gpsimd.affine_select(out=ident[:, :], in_=ident[:, :], compare_op=ALU.not_equal, fill=1.0, base=0,
                                    pattern=[[-1, 128]], channel_multiplier=1).then_inc(s_consts, 1)
            ordered(nc.gpsimd.memset(gate_mask[:, :, :], 0.0))
            ordered(nc.gpsimd.memset(b_scale[:, :], 0.5))
            for r in (0, 32):
                ordered(nc.gpsimd.affine_select(out=gate_mask[:, :, :], in_=gate_mask[:, :, :], compare_op=ALU.not_equal,
                                                fill=1.0, base=-r, pattern=[[-1, GATES], [0, 128]], channel_multiplier=1))
                ordered(nc.gpsimd.affine_select(out=b_scale[:, :], in_=b_scale[:, :], compare_op=ALU.not_equal,
                                                fill=1.0, base=-(r + GATES - 1), pattern=[[0, 1]], channel_multiplier=1))
            ordered(nc.gpsimd.memset(gates[0][:, GATES, :], 0.0))
            nc.gpsimd.memset(ones[:, :], 1.0).then_inc(s_consts, 1)
            ordered(nc.gpsimd.memset(before[:, :, :], 1.0))
            ordered(nc.gpsimd.affine_select(out=before[:, :, :], in_=before[:, :, :], compare_op=ALU.is_gt,
                                            fill=0.0, base=0, pattern=[[1, E], [-1, E]], channel_multiplier=0))
            nc.gpsimd.memset(minus_half[:, :], -0.5).then_inc(s_consts, 1)
            pool.wait_ge(s_consts, 3)

            def segment(g):
                for l in g.steps:
                    if l == g.stats_at:
                        pool.wait_ge(s_var, g.lstm + 1)
                        nc.gpsimd.tensor_tensor(rms[:, :], var[:, :], minus_half[:, :], ALU.pow).then_inc(s_rms, 1)
                        pool.wait_ge(s_rms, g.lstm + 1)
                        pool.wait_ge(s_raw, g.lstm + 1)
                        nc.gpsimd.tensor_tensor(logits[:, :, :], raw_logits[:, :, :],
                                                rms[:, :].unsqueeze(2).broadcast_to([128, NG, E]), ALU.mult).then_inc(s_logits, 1)
                    for n in g.weighed_at(l):
                        if n > 0:
                            pool.wait_ge(s_wt, g.ffn * X + n + 1)
                            wait(pool, s_acc, g.ffn * E + n - 1)
                            nc.gpsimd.tensor_tensor(acc[:, :], acc[:, :], weighted[n % 2][:, :], ALU.add).then_inc(s_acc, 1)
                    if l == g.scale_at:
                        pool.wait_ge(s_route, g.lstm * ROUTE + 2)
                        nc.gpsimd.tensor_tensor(equal[:, :, :, :], equal[:, :, :, :],
                                                before[:, :, :].unsqueeze(1).broadcast_to([128, NG, E, E]), ALU.mult).then_inc(s_masked, 1)
                        pool.wait_ge(s_masked, g.lstm * 2 + 1)
                        nc.gpsimd.tensor_tensor(above[:, :, :, :], above[:, :, :, :], equal[:, :, :, :], ALU.add).then_inc(s_masked, 1)

            run(pool, segment)

        @block.scalar
        def _(act):
            act.dma_start(wx_raw[:, :], Wx).then_inc(s_wlstm, 16)
            act.dma_start(wh_raw[:, :], Wh).then_inc(s_wlstm, 16)
            act.wait_ge(s_zeroed, 1)
            for r in (0, 32):
                act.dma_start(b_rows[r:r + GATES, :], b.rearrange("(g p) -> g p", p=128)).then_inc(s_brow, 16)
            act.wait_ge(s_wlstm, 32)
            S = (GATES - 1) * D
            nc.scalar.mul(wx[:, 0:S], wx_raw[:, 0:S], 0.5)
            nc.scalar.mul(wx[:, S:], wx_raw[:, S:], 1.0)
            nc.scalar.mul(wh[:, 0:S], wh_raw[:, 0:S], 0.5 / H_SCALE)
            nc.scalar.mul(wh[:, S:], wh_raw[:, S:], 1.0 / H_SCALE).then_inc(s_wx, 1)

            def squares(g, k):
                act.wait_ge(s_hs, g.step(GS * (k + 1)))
                if k == 0 and not g.first:
                    act.wait_ge(s_copied, g.lstm)
                cols = slice(k * 128, (k + 1) * 128)
                nc.scalar.activation(h_sq[:, cols], hs[:, cols], ACT.Square).then_inc(s_sq, 1)

            def relu(g, j):
                J = g.ffn * TILES + j
                act.wait_ge(s_z, J + 1)
                wait(act, s_l2, J - RING + 1)
                bias = params[:, ROW_B1 + j:ROW_B1 + j + 1]
                if j % 2 == 0:
                    nc.scalar.activation(h_hi[j % RING][:, :], z_ps[j % ZB][:, :], ACT.Relu, bias=bias)
                nc.scalar.activation(h_full[j % RING][:, :], z_ps[j % ZB][:, :], ACT.Relu, bias=bias).then_inc(s_hf, 1)

            def segment(g):
                for l in g.steps:
                    if g.has_step(l):
                        s = g.step(l)
                        act.wait_ge(s_gates, s + 1)
                        nc.scalar.activation(gates[l % 2][:, 0:GATES, :],
                                             gate_ps[(l // GS) % 2][:, :].rearrange("p (g t n) -> p g t n", g=GATES, n=N)[:, :, l % GS, :],
                                             ACT.Tanh).then_inc(s_gates_act, 1)
                    if not g.tail and l % GS == 0 and GS <= l <= STEPS:
                        squares(g, l // GS - 1)
                    for j in g.held_back(l - 1):
                        relu(g, j)
                    if g.has_step(l):
                        act.wait_ge(s_c, s + 1)
                        nc.scalar.activation(tanh_c[:, :], gates[(l + 1) % 2][:, GATES, :], ACT.Tanh, scale=0.5).then_inc(s_tanh_c, 1)
                    if g.first and l < 2 * X:
                        n, w = l // 2, l % 2
                        act.wait_ge(s_w[n], 32)
                        nc.scalar.copy(w_hi[:, n, w, :], w_raw[n % WRING][:, w, :]).then_inc(s_w_hi, 1)
                    for j in g.taken_on(l):
                        relu(g, j)
                    if l == g.scale_at:
                        act.wait_ge(s_logits, g.lstm + 1)
                        nc.scalar.activation(probs[:, :, :], logits[:, :, :], ACT.Sigmoid).then_inc(s_probs, 1)

            run(act, segment)

        @block.vector
        def _(dve):
            setup = [0]

            def ordered(ins):
                setup[0] += 1
                ins.then_inc(s_setup, 1)
                dve.wait_ge(s_setup, setup[0])

            dve.wait_ge(s_spare, intro.use("params") + 1)
            ordered(nc.vector.tensor_copy(params[:, :], spare_ps[:, 0:ROWS]))
            nc.vector.tensor_scalar(h_init[:, :], params[:, ROW_H0:ROW_H0 + N], H_SCALE, None, ALU.mult).then_inc(s_spare_read, 1)
            ordered(nc.vector.tensor_scalar(nw_scaled[:, :], params[:, ROW_NW:ROW_NW + 1], 1.0 / H_SCALE, None, ALU.mult))
            dve.wait_ge(s_spare, intro.use("xt", 0) + 1)
            nc.vector.tensor_copy(x_t[:, :], spare_ps[:, 0:128]).then_inc(s_spare_read, 1)
            dve.wait_ge(s_brow, 32)
            dve.wait_ge(s_consts, 3)
            ordered(nc.vector.tensor_scalar(b_scaled[:, :], b_rows[:, :], b_scale[:, 0:1], None, ALU.mult))
            ordered(nc.vector.tensor_copy(b_round[:, :], b_scaled[:, :]))
            nc.vector.tensor_copy(gate_maskr[:, :, :], gate_mask[:, :, :])
            nc.vector.tensor_copy(b_parts[0:32, :], b_scaled[0:32, :])
            ordered(nc.vector.tensor_tensor(b_parts[32:64, :], b_scaled[32:64, :], b_round[32:64, :].bitcast(F32), ALU.subtract))
            ordered(nc.vector.tensor_scalar(rw_scaled[:, :], params[:, ROW_RW:ROW_RW + E], nw_scaled[:, 0:1], None, ALU.mult))
            assert setup[0] == SETUP
            n = [0]

            def split3(parts, rest, whole):
                def step(ins):
                    n[0] += 1
                    ins.then_inc(s_wh, 1)
                    dve.wait_ge(s_wh, n[0])

                step(nc.vector.tensor_copy(parts[:, 0, :], whole))
                step(nc.vector.tensor_tensor(rest[:, 0, :], whole, parts[:, 0, :], ALU.subtract))
                step(nc.vector.tensor_copy(parts[:, 1, :], rest[:, 0, :]))
                step(nc.vector.tensor_tensor(rest[:, 1, :], rest[:, 0, :], parts[:, 1, :], ALU.subtract))
                step(nc.vector.tensor_copy(parts[:, 2, :], rest[:, 1, :]))

            dve.wait_ge(s_wx, 1)
            split3(wh_parts, wh_rest, wh[:, :])
            split3(rw_parts, rw_rest, rw_scaled[:, :])
            assert n[0] == 2 * SPLIT3

            def split(g, j):
                J = g.ffn * TILES + j
                dve.wait_ge(s_hf, J + 1)
                if j % 2:
                    nc.vector.tensor_copy(h_hi[j % RING][:, :], h_full[j % RING][:, :]).then_inc(s_hi, 1)
                    dve.wait_ge(s_hi, g.ffn * (TILES // 2) + j // 2 + 1)
                nc.vector.tensor_tensor(h_lo[j % RING][:, :], h_full[j % RING][:, :],
                                        h_hi[j % RING][:, :].bitcast(F32), ALU.subtract).then_inc(s_lo, 1)

            def weigh(g, n):
                dve.wait_ge(s_l2, g.ffn * TILES + (n + 1) * KT)
                b2 = params[:, ROW_B2 + n:ROW_B2 + n + 1]
                if n == 0:
                    nc.vector.tensor_scalar(acc[:, :], eo_ps[0][:, :], b2, None, ALU.add).then_inc(s_wt, 1)
                else:
                    dve.wait_ge(s_bc[(n - 1) // (E // 2)], (g.ffn + 1) * 16)
                    wait(dve, s_acc, g.ffn * E + n - 2)
                    nc.vector.scalar_tensor_tensor(weighted[n % 2][:, :], eo_ps[n % 2][:, :], b2, comb_bc[:, n - 1, :],
                                                   ALU.add, ALU.mult).then_inc(s_wt, 1)

            def final(ffn, use):
                dve.wait_ge(s_spare, use + 1)
                dve.wait_ge(s_res, 16 * GS * (ffn + 1))
                wait(dve, s_out, 16 * GS * ffn)
                nc.vector.tensor_tensor(out_sb[:, :, :], spare_ps[:, :].rearrange("p (g d) -> p g d", g=NG),
                                        x_res[:, :, :], ALU.add).then_inc(s_spare_read, 1)

            def split_xn(g):
                c = g.lstm
                dve.wait_ge(s_spare_read, g.use("scale") + 1)
                wait(dve, s_z, c * TILES)
                nc.vector.tensor_copy(xn_hi[:, :], xn[:, :]).then_inc(s_xhi, 1)
                dve.wait_ge(s_xhi, c + 1)
                nc.vector.tensor_tensor(xn_lo[:, :], xn[:, :], xn_hi[:, :].bitcast(F32), ALU.subtract).then_inc(s_xlo, 1)

            def compare(g):
                dve.wait_ge(s_probs, g.lstm + 1)
                other = probs[:, :, :].unsqueeze(2).broadcast_to([128, NG, E, E])
                own = probs[:, :, :].unsqueeze(3).broadcast_to([128, NG, E, E])
                nc.vector.tensor_tensor(above[:, :, :, :], other, own, ALU.is_gt).then_inc(s_route, 1)
                nc.vector.tensor_tensor(equal[:, :, :, :], other, own, ALU.is_equal).then_inc(s_route, 1)

            def choose(c):
                n = [2]

                def ordered(ins):
                    n[0] += 1
                    ins.then_inc(s_route, 1)
                    dve.wait_ge(s_route, c * ROUTE + n[0])

                dve.wait_ge(s_masked, (c + 1) * 2)
                ordered(nc.vector.tensor_reduce(rank[:, :, :], above[:, :, :, :], AX.X, ALU.add))
                ordered(nc.vector.scalar_tensor_tensor(chosen[:, :, :], rank[:, :, :], 1.5, probs[:, :, :], ALU.is_lt, ALU.mult))
                ordered(nc.vector.tensor_reduce(total[:, :], chosen[:, :, :], AX.X, ALU.add))
                ordered(nc.vector.tensor_scalar(total_inv[:, :], total[:, :], EPS_TOP, None, ALU.add))
                ordered(nc.vector.reciprocal(total[:, :], total_inv[:, :]))
                nc.vector.tensor_tensor(comb[:, :, :].rearrange("p e g -> p g e"), chosen[:, :, :],
                                        total[:, :].unsqueeze(2).broadcast_to([128, NG, E]), ALU.mult).then_inc(s_comb, 1)
                assert n[0] == ROUTE

            def segment(g):
                for l in g.steps:
                    if g.has_step(l):
                        s, now, nxt = g.step(l), gates[l % 2], gates[(l + 1) % 2]
                        dve.wait_ge(s_gates_act, s + 1)
                        wait(dve, s_c, s)
                        nc.vector.scalar_tensor_tensor(uv[:, :, :], now[:, 0:2, :], 1.0, now[:, 3:5, :], ALU.add, ALU.mult).then_inc(s_uv, 1)
                        dve.wait_ge(s_uv, s + 1)
                        nc.vector.scalar_tensor_tensor(nxt[:, GATES, :], uv[:, 1, :], 0.5, uv[:, 0, :], ALU.mult, ALU.add).then_inc(s_c, 1)
                        nc.vector.tensor_scalar(o_scaled[:, :], now[:, 2, :], 1.0, H_SCALE / 2, ALU.add, ALU.mult).then_inc(s_o, 1)
                    for j in g.held_back(l - 1):
                        split(g, j)
                    if g.has_step(l):
                        dve.wait_ge(s_tanh_c, s + 1)
                        dve.wait_ge(s_o, s + 1)
                        cols = slice(l * N, (l + 1) * N)
                        nc.vector.tensor_tensor(h_a[:, cols], o_scaled[:, :], tanh_c[:, :], ALU.mult).then_inc(s_ha, 1)
                        nc.vector.tensor_tensor(hs[:, cols], o_scaled[:, :], tanh_c[:, :], ALU.mult).then_inc(s_hs, 1)
                        dve.wait_ge(s_hs, s + 1)
                        nc.vector.tensor_tensor(h_b[:, cols], hs[:, cols], h_a[:, cols], ALU.subtract).then_inc(s_h, 1)
                    if g.transposes_x(l):
                        wait(dve, s_spare, g.use("xt", l // GS + 1) + 1)
                        nc.vector.tensor_copy(x_t[:, :], spare_ps[:, 0:128]).then_inc(s_spare_read, 1)
                    if l == g.stats_at:
                        dve.wait_ge(s_spare, g.use("stats") + 1)
                        nc.vector.tensor_copy(stats[:, :, :], spare_ps[:, 0:NG * (1 + 3 * E)].rearrange("p (g k) -> p g k", g=NG)).then_inc(s_spare_read, 1)
                        dve.wait_ge(s_spare_read, g.use("stats") + 1)
                        nc.vector.tensor_scalar(var[:, :], stats[:, :, 0], 1.0 / (D * H_SCALE * H_SCALE), EPS_RMS, ALU.mult, ALU.add).then_inc(s_var, 1)
                        nc.vector.tensor_reduce(raw_logits[:, :, :], stats[:, :, 1:].rearrange("p g (k e) -> p g e k", k=3),
                                                AX.X, ALU.add).then_inc(s_raw, 1)
                    if l == g.scale_at:
                        dve.wait_ge(s_spare, g.use("scale") + 1)
                        nc.vector.scalar_tensor_tensor(xn[:, :], hs[:, 0:TOK], nw_scaled[:, 0:1], spare_ps[:, :], ALU.mult, ALU.mult).then_inc(s_spare_read, 1)
                    if l == g.start + 1 and g.has_final:
                        final(g.ffn - 1, g.use("final"))
                    if g.first and l < 2 * X:
                        n, w = l // 2, l % 2
                        dve.wait_ge(s_w_hi, l + 1)
                        nc.vector.tensor_tensor(w_lo[:, n, w, :], w_raw[n % WRING][:, w, :], w_hi[:, n, w, :].bitcast(F32), ALU.subtract).then_inc(s_w_split, 1)
                    for j in g.taken_on(l):
                        split(g, j)
                    if l == g.scale_at:
                        split_xn(g)
                    if l == g.end - 1 and g.has_step(l):
                        lead = (g.end - STEPS) * N
                        dve.wait_ge(s_h, g.step(l) + 1)
                        for state in (h_a, h_b, hs):
                            last = nc.vector.tensor_copy(state[:, 0:lead], state[:, TOK:TOK + lead])
                        last.then_inc(s_copied, 1)
                    if l == g.start and g.ffn is not None:
                        choose(g.ffn)
                    if l == g.start + 1 and g.ffn is not None:
                        dve.wait_ge(s_spare, g.use("comb") + 1)
                        nc.vector.tensor_copy(comb_rows[:, :], spare_ps[0:E * NG, 0:128]).then_inc(s_spare_read, 1)
                    for n in g.weighed_at(l):
                        weigh(g, n)
                    if l == g.scale_at:
                        compare(g)

            run(dve, segment)
            final(CHUNKS - 1, FINAL_USE)

        @block.tensor
        def _(pe):
            def to_spare(g_use):
                wait(pe, s_spare_read, g_use)

            def transpose_x(q_slot, q_use, waits):
                pe.wait_ge(s_x[q_slot], waits)
                to_spare(q_use)
                nc.tensor.transpose(spare_ps[:, 0:128], x_group[q_slot][:, :], ident[:, :]).then_inc(s_spare, 1)

            def prime(q_bank):
                bank = gate_ps[q_bank]
                nc.tensor.matmul(bank[:, :], b_parts[:, :], gate_maskr[:, :, :].rearrange("p g c -> p (g c)"), start=True, stop=False,
                                 skip_group_check=True)
                for k in range(GATES):
                    nc.tensor.matmul(bank[:, k * 128:(k + 1) * 128], wx[:, k * D:(k + 1) * D], x_t[:, :], start=False, stop=False,
                                     skip_group_check=True)

            def lstm_step(g, l):
                s = g.step(l)
                bank = gate_ps[(l // GS) % 2]
                if g.first and l == 0:
                    for k in range(GATES):
                        c0 = k * 128
                        last = nc.tensor.matmul(bank[:, c0:c0 + N], wh[:, k * D:(k + 1) * D], h_init[:, :], start=False, stop=False,
                                                skip_group_check=True)
                    last.then_inc(s_gates, 1)
                    return
                if g.first and l == 1:
                    pe.wait_ge(s_wh, SPLIT3)
                prev = l - 1 if l > g.start else g.before - 1
                cols = slice(prev * N, (prev + 1) * N)
                wait(pe, s_ha, s)
                for h, parts in ((h_a, (0, 1, 2)), (h_b, (0, 1))):
                    for k in range(GATES):
                        c0 = k * 128 + (l % GS) * N
                        for w in parts:
                            if h is h_b and k == 0 and w == 0:
                                wait(pe, s_h, s)
                            last = nc.tensor.matmul(bank[:, c0:c0 + N], wh_parts[:, w, k * D:(k + 1) * D], h[:, cols], start=False,
                                                    stop=(l % GS == GS - 1), skip_group_check=True)
                last.then_inc(s_gates, 1)

            def layer1(g, j):
                J = g.ffn * TILES + j
                n, k = j // KT, j % KT
                if j == 0:
                    pe.wait_ge(s_xlo, g.ffn + 1)
                wait(pe, s_hf, J - ZB + 1)
                if isinstance(g.ffn, int) and g.ffn == 0 and k == 0:
                    pe.wait_ge(s_w_split, 2 * n + 1)
                z, cols = z_ps[j % ZB][:, :], slice(k * 128, (k + 1) * 128)
                nc.tensor.matmul(z, w_hi[:, n, 0, cols], xn_hi[:, :], start=True, stop=False)
                nc.tensor.matmul(z, w_lo[:, n, 0, cols], xn_hi[:, :], start=False, stop=False)
                nc.tensor.matmul(z, w_hi[:, n, 0, cols], xn_lo[:, :], start=False, stop=True).then_inc(s_z, 1)

            def layer2(g, j):
                J = g.ffn * TILES + j
                n, k = j // KT, j % KT
                pe.wait_ge(s_lo, J + 1)
                if k == 0:
                    wait(pe, s_wt, g.ffn * X + (n - 1 if n else 0))
                if isinstance(g.ffn, int) and g.ffn == 0 and k == 0:
                    pe.wait_ge(s_w_split, 2 * n + 2)
                eo, cols = eo_ps[n % 2][:, :], slice(k * 128, (k + 1) * 128)
                nc.tensor.matmul(eo, w_hi[:, n, 1, cols], h_hi[j % RING][:, :], start=(k == 0), stop=False)
                nc.tensor.matmul(eo, w_lo[:, n, 1, cols], h_hi[j % RING][:, :], start=False, stop=False)
                nc.tensor.matmul(eo, w_hi[:, n, 1, cols], h_lo[j % RING][:, :], start=False, stop=(k == KT - 1)).then_inc(s_l2, 1)

            def broadcast_columns(src):
                for k in range(NG):
                    last = nc.tensor.transpose(spare_ps[:, k * 128:(k + 1) * 128], src(k).broadcast_to([128, 128]), ident[:, :])
                last.then_inc(s_spare, 1)

            def final(ffn, use):
                pe.wait_ge(s_acc, E * (ffn + 1))
                to_spare(use)
                for k in range(NG):
                    last = nc.tensor.transpose(spare_ps[:, k * 128:(k + 1) * 128], acc[:, k * 128:(k + 1) * 128], ident[:, :])
                last.then_inc(s_spare, 1)

            def segment(g):
                if g.first:
                    pe.wait_ge(s_consts, 1)
                    pe.wait_ge(s_params_in, 7 * 16)
                    nc.tensor.transpose(spare_ps[:, 0:ROWS], params_in[:, :], ident[0:ROWS, 0:ROWS]).then_inc(s_spare, 1)
                    transpose_x(0, g.use("xt", 0), 16 * GS)
                    pe.wait_ge(s_setup, SETUP)
                    pe.wait_ge(s_wx, 1)
                    wait(pe, s_spare_read, g.use("xt", 0) + 1)
                    prime(0)
                for l in g.steps:
                    k = l // GS + 1
                    if g.has_step(l):
                        lstm_step(g, l)
                    if g.transposes_x(l):
                        transpose_x(k % 2, g.use("xt", k), (g.lstm * (NG // 2) + k // 2 + 1) * (16 * GS))
                    if g.primes(l):
                        if ("xt", k) in g.spare:
                            wait(pe, s_spare_read, g.use("xt", k) + 1)
                        prime(k % 2)
                    if l == g.stats_at:
                        pe.wait_ge(s_sq, NG * (g.lstm + 1))
                        if g.first:
                            pe.wait_ge(s_wh, 2 * SPLIT3)
                        to_spare(g.use("stats"))
                        for q in range(NG):
                            cols, c0 = slice(q * 128, (q + 1) * 128), q * (1 + 3 * E)
                            nc.tensor.matmul(spare_ps[:, c0:c0 + 1], h_sq[:, cols], ones[:, :], start=True, stop=True)
                            parts = rw_parts[:, :, :].rearrange("p k e -> p (k e)")
                            nc.tensor.matmul(spare_ps[:, c0 + 1:c0 + 1 + 3 * E], h_a[:, cols], parts, start=True, stop=False)
                            last = nc.tensor.matmul(spare_ps[:, c0 + 1:c0 + 1 + 3 * E], h_b[:, cols], parts, start=False, stop=True)
                        last.then_inc(s_spare, 1)
                    if l == g.scale_at:
                        pe.wait_ge(s_rms, g.lstm + 1)
                        to_spare(g.use("scale"))
                        broadcast_columns(lambda k: rms[:, k:k + 1])
                    if l == g.start + 1 and g.has_final:
                        final(g.ffn - 1, g.use("final"))
                    if g.ffn is not None and l == g.start:
                        for j in range(LAG):
                            layer1(g, j)
                    for j in g.tiles_at(l):
                        if j + LAG < TILES:
                            layer1(g, j + LAG)
                        layer2(g, j)
                    if l == g.start + 1 and g.ffn is not None:
                        pe.wait_ge(s_comb, g.ffn + 1)
                        to_spare(g.use("comb"))
                        nc.tensor.transpose(spare_ps[0:E * NG, 0:128], comb[:, :, :].rearrange("p e g -> p (e g)"), ident[:, :]).then_inc(s_spare, 1)

            run(pe, segment)
            final(CHUNKS - 1, FINAL_USE)


_INS = ['x', 'cond_1024', 'L0_cond_Wx', 'L0_cond_Wh', 'L0_cond_b', 'L0_ffn_norm_weight', 'L0_ffn_router_w', 'L0_ffn_sw1',
        'L0_ffn_sb1', 'L0_ffn_sw2', 'L0_ffn_sb2', 'L0_ffn_ew1', 'L0_ffn_eb1', 'L0_ffn_ew2', 'L0_ffn_eb2']
_OUTS = [((N, T, D), 'float32')]


def kernel(**inputs):
    import numpy as _np
    import concourse.bacc as _bacc
    from concourse import mybir as _mybir
    from concourse.bass_utils import run_bass_kernel_spmd as _run

    nc = _bacc.Bacc("TRN2", target_bir_lowering=False, num_devices=1)
    arrays, args = {}, []
    for name in _INS:
        a = _np.ascontiguousarray(inputs[name])
        arrays[f"in_{name}_dram"] = a
        args.append(nc.dram_tensor(f"in_{name}_dram", a.shape, _mybir.dt.from_np(a.dtype), kind="ExternalInput").ap())
    for i, (shape, dtype) in enumerate(_OUTS):
        dt = _mybir.dt.from_np(_np.dtype(dtype))
        args.append(nc.dram_tensor(f"out_{i}_dram", shape, dt, kind="ExternalOutput").ap())
    adaln_ffn_kernel(nc, *args)
    r = _run(nc, [arrays], core_ids=[0])
    return r.results[0]["out_0_dram"]
```

```python
import concourse.bass as bass
from concourse import mybir
from contextlib import ExitStack

F32 = mybir.dt.float32
F32R = mybir.dt.float32r
I32 = mybir.dt.int32
BF16 = mybir.dt.bfloat16
F16 = mybir.dt.float16
ALU = mybir.AluOpType
ACT = mybir.ActivationFunctionType
AX = mybir.AxisListType

N = 32
T = 128
D = 128
HID = 512
E = 8
X = E + 1
KT = HID // 128
GATES = 4
GS = 128 // N
STEPS = 16
TOK = STEPS * N
NG = STEPS // GS
CHUNKS = T // STEPS + 1
TILES = X * KT
LEAD = 4
LAG = 3
ZB = 3
OPEN = LAG + 1
OPEN_WEIGHT = 1
POOL_LO = [*range(0, 32, 2)]
WRING = 5
RING = 6
H_SCALE = 2.0 ** 12
WH_SCALE = 2.0 ** 14
WH_LEAST = 2.0 ** -40
EPS_RMS = 1e-8
EPS_TOP = 1e-6

ROW_B1 = 0
ROW_B2 = ROW_B1 + TILES
ROW_NW = ROW_B2 + X
ROW_RW = ROW_NW + 1
ROWS = ROW_RW + E


def steps_in(c):
    return STEPS // 2 if isinstance(c, int) and c in (0, CHUNKS - 1) else STEPS


def tokens(c):
    return steps_in(c) * N


def groups(c):
    return steps_in(c) // GS


def first_step(c):
    return 0 if isinstance(c, int) and c == 0 else c * STEPS - STEPS // 2


def lo_on_pool(c, j):
    return isinstance(c, int) and c == 0 and j in POOL_LO


def lo_done(c, j):
    if isinstance(c, int) and c == 0:
        return sum(i not in POOL_LO for i in range(j + 1))
    return c * TILES - len(POOL_LO) + j + 1


def first_group(c):
    return 0 if isinstance(c, int) and c == 0 else c * NG - NG // 2


def wait(eng, sem, value):
    if not isinstance(value, int) or value > 0:
        eng.wait_ge(sem, value)


class Segment:

    def __init__(self, ffn, lstm, base, start=LEAD, lead=LEAD, last=False, has_final=True):
        self.ffn, self.lstm, self.base = ffn, lstm, base
        self.first, self.last, self.tail = ffn is None, last, lstm is None
        self.has_final = has_final
        self.lstm_bound = isinstance(ffn, int) and ffn == 0
        self.size = STEPS if lstm is None else steps_in(lstm)
        self.start, self.end = start, self.size + lead
        self.before = (steps_in(ffn) if ffn is not None else 0) + start
        self.steps = range(start, self.end)
        self.stats_at, self.scale_at = (None, None) if self.tail else (self.size, self.size + 1)
        later = 0 if self.first else 1
        self.take_stats_at, self.take_scale_at = (None, None) if self.tail else (self.size + later, self.size + 1 + later)
        self.split_xn_at = None if self.tail else self.size + 1 if self.first else self.end - 2
        self.copy_at = start + 1 if (ffn is not None and steps_in(ffn) < STEPS) or self.size < STEPS else 2 * GS
        self.squares_at = [STEPS - 6, STEPS - 4, STEPS - 2, STEPS] if self.size == STEPS else [self.size - 2, self.size]
        self.spare = []
        if self.first:
            self.spare += ["x_first", "params"]
        for l in self.steps:
            if self.transposes_x(l):
                self.spare.append("x_next")
            if l == self.stats_at:
                self.spare.append("stats")
            if l == self.scale_at:
                self.spare.append("scale")
            if l == start + 1 and ffn is not None:
                self.spare.append("comb")
            if l == start + 3 and has_final:
                self.spare.append("final")

    def tiles_at(self, l):
        if self.ffn is None or l < self.start:
            return range(0)
        work = [j + sum(OPEN <= k + LAG < TILES for k in range(j)) for j in range(TILES)]
        n = self.end - self.start
        per_step = max((2 * TILES - OPEN + OPEN_WEIGHT) / n, (work[TILES - LAG - 1] + 1) / (n - 1))
        return [j for j in range(TILES) if int(work[j] / per_step) == l - self.start]

    def first_layer(self, l):
        return [j + LAG for j in self.tiles_at(l) if OPEN <= j + LAG < TILES]

    def held_back(self, l):
        return [] if self.lstm_bound else [j for j in self.first_layer(l)[-1:] if j < TILES - 1]

    def beside(self, l):
        return self.held_back(l - 1) + ([2] if self.ffn is not None and l == self.start and not self.lstm_bound else [])

    def taken_on(self, l):
        opened = range(2 if self.lstm_bound else 3, OPEN) if self.ffn is not None and l == self.start else []
        return [*opened, *(j for j in self.first_layer(l) if j not in self.held_back(l))]

    def weighed_at(self, l):
        return [j // KT - 1 for j in self.tiles_at(l) if j >= KT and j % KT == 0]

    def opens(self, l):
        return not self.tail and l == self.end - 1

    def has_step(self, l):
        return not self.tail and not (self.last and l >= self.size)

    def transposes_x(self, l):
        return not self.tail and not self.last and l == self.size - GS

    def starts_gates(self, l):
        return not self.tail and l % GS == 1 and not (self.last and l // GS + 1 >= self.size // GS)

    def primes(self, l):
        k = l // GS + 1
        if self.tail or (self.last and k >= self.size // GS) or l % GS not in (2, 3):
            return None
        return k, range(0, 2) if l % GS == 2 else range(2, GATES)

    def use(self, name):
        return self.base + self.spare.index(name)

    def step(self, l):
        return first_step(self.lstm) + l


def adaln_ffn_kernel(nc, x, cond, Wx, Wh, b, nw, rw, sw1, sb1, sw2, sb2, ew1, eb1, ew2, eb2, out):
    ctx = ExitStack()
    with ctx:
        def sb(name, shape, dt=F32):
            return ctx.enter_context(nc.sbuf_tensor(name, shape, dt))

        def ps(name):
            return ctx.enter_context(nc.psum_tensor(name, [128, 512], F32))

        def sem(name):
            return ctx.enter_context(nc.semaphore(name))

        x_chunk = sb("x_chunk", [128, GS, D])
        x_t = sb("x_t", [D, TOK])
        x_res = sb("x_res", [128, GS, D])
        out_sb = sb("out_sb", [128, GS, D])
        wx_raw, wh_raw = sb("wx_raw", [D, GATES * D]), sb("wh_raw", [D, GATES * D])
        wx, wh = sb("wx", [D, GATES * D]), sb("wh", [D, GATES * D])
        wh_parts = sb("wh_parts", [D, 2, GATES * D], F16)
        row_max, wh_max = sb("row_max", [D, 1]), sb("wh_max", [D, 1])
        wh_top = sb("wh_top", [D, 1])
        wh_top_inv = sb("wh_top_inv", [D, 1])
        unit = sb("unit", [D, 5])
        b_cols = sb("b_cols", [128, GATES])
        opener = sb("opener", [128, 512], F16)
        gates = [sb(f"gates{s}", [128, GATES + 1, N]) for s in range(2)]
        uv = sb("uv", [128, 2, N])
        tanh_c = sb("tanh_c", [128, N])
        o_scaled = sb("o_scaled", [128, N])
        hs = sb("hs", [128, (STEPS + LEAD) * N])
        h_a, h_b = sb("h_a", [128, (STEPS + LEAD) * N], F16), sb("h_b", [128, (STEPS + LEAD) * N], F16)
        rw_parts = sb("rw_parts", [128, 3, E], BF16)
        rw_rest = sb("rw_rest", [128, 2, E])
        h_sq = sb("h_sq", [128, TOK])
        params_in = sb("params_in", [ROWS, D])
        params = sb("params", [D, ROWS])
        given = sb("given", [N + GATES, D])
        h_init = sb("h_init", [128, N])
        nw_scaled = sb("nw_scaled", [128, 1])
        rw_scaled = sb("rw_scaled", [128, E])
        ident, ones = sb("ident", [128, 128]), sb("ones", [128, 1])
        before = sb("before", [128, E, E])
        minus_half = sb("minus_half", [128, NG])
        stats = sb("stats", [128, NG, 1 + 3 * E])
        raw_logits = sb("raw_logits", [128, NG, E])
        var, rms = sb("var", [128, NG]), sb("rms", [128, NG])
        logits, probs = sb("logits", [128, NG, E]), sb("probs", [128, NG, E])
        above, equal = sb("above", [128, NG, E, E]), sb("equal", [128, NG, E, E])
        rank, chosen = sb("rank", [128, NG, E]), sb("chosen", [128, NG, E])
        total_eps, eps_top, minus_one = (sb(name, [128, NG]) for name in ("total_eps", "eps_top", "minus_one"))
        total, total_inv = sb("total", [128, NG]), sb("total_inv", [128, NG])
        comb = sb("comb", [128, E * NG])
        comb_rows = sb("comb_rows", [E * NG, 128])
        comb_bc = sb("comb_bc", [128, E * TOK])
        xn = sb("xn", [128, TOK])
        xn_hi, xn_lo = sb("xn_hi", [128, TOK], F32R), sb("xn_lo", [128, TOK], F32R)
        w_raw = [sb(f"w_raw{x_}", [128, 2, HID]) for x_ in range(WRING)]
        w_hi = sb("w_hi", [128, X, 2, HID], F32R)
        w_lo = sb("w_lo", [128, X, 2, HID], F32R)
        h_full = [sb(f"h_full{s}", [128, TOK]) for s in range(RING)]
        h_hi = [sb(f"h_hi{s}", [128, TOK], F32R) for s in range(RING)]
        h_lo = [sb(f"h_lo{s}", [128, TOK], F32R) for s in range(RING)]
        weighted = [sb(f"weighted{s}", [128, TOK]) for s in range(2)]
        acc = sb("acc", [128, TOK])
        summed = sb("summed", [128, TOK])

        gate_ps = [ps(f"gate_ps{s}") for s in range(2)]
        z_ps = [ps(f"z_ps{s}") for s in range(ZB)]
        eo_ps = [ps(f"eo_ps{s}") for s in range(2)]
        spare_ps = ps("spare_ps")

        s_consts = sem("consts")
        s_const_step = sem("const_step")
        s_params_in = sem("params_in_dma")
        s_wx_in, s_wh_in = sem("wx_dma"), sem("wh_dma")
        s_w = [sem(f"w_dma{x_}") for x_ in range(X)]
        s_x = sem("x_chunk_dma")
        s_given_in = sem("given_dma")
        s_res = sem("x_res_dma")
        s_out = sem("out_dma")
        s_setup_ps = sem("setup_transposed")
        s_opened = sem("gate_banks_opened")
        s_zero_c = sem("cell_zeroed")
        s_bcols = sem("b_cols_done")
        s_given = sem("h_init_done")
        s_bias = sem("bias_in_bank")
        s_params = sem("params_done")
        s_row_max = sem("row_max_done")
        s_unit = sem("unit_done")
        s_wx = sem("wx_scaled")
        s_spare = sem("spare_written")
        s_spare_read = sem("spare_read")
        s_gates = sem("gates_summed")
        s_gates_act = sem("gates_tanh")
        s_uv = sem("uv_done")
        s_c = sem("cell_done")
        s_tanh_c = sem("tanh_c_done")
        s_o = sem("o_scaled_done")
        s_ha = sem("h_a_done")
        s_hs = sem("hs_done")
        s_wh = sem("wh_split")
        s_h = sem("h_done")
        s_w_hi = sem("w_hi_done")
        s_w1_split = sem("w1_split_done")
        s_w2_split = sem("w2_split_done")
        s_z = sem("z_done")
        s_hf = sem("h_full_done")
        s_hi = sem("h_hi_done")
        s_lo = sem("h_lo_done")
        s_pool_lo = sem("pool_h_lo_done")
        s_l2 = sem("h_used")
        s_wt = sem("weighted_done")
        s_acc = sem("acc_done")
        s_sq = sem("h_sq_done")
        s_copied = sem("lead_copied")
        s_raw = sem("raw_logits_done")
        s_var = sem("var_done")
        s_rms = sem("rms_done")
        s_logits = sem("logits_done")
        s_probs = sem("probs_done")
        s_route = sem("route_step")
        s_xhi = sem("xn_hi_done")
        s_xlo = sem("xn_lo_done")
        s_comb = sem("comb_done")
        s_total = sem("total_done")
        s_norm = sem("comb_step")
        s_masked = sem("ties_masked")
        s_row = sem("comb_rows_dma")
        s_bc = [sem(f"comb_bc_dma{s}") for s in range(2)]
        ROUTE = 4
        UNITS = 9
        UNIT_WH, UNIT_WH_HALF, UNIT_WX, UNIT_WX_HALF, UNIT_TANH = range(5)
        WH_STEPS = 3
        PARAM_STEPS = 7

        block = ctx.enter_context(nc.Block())

        FIRST_LEAD = 2
        intro = Segment(None, 0, 0, start=0, lead=FIRST_LEAD, has_final=False)
        early = Segment(0, 1, len(intro.spare), start=FIRST_LEAD, has_final=False)
        second = Segment(1, 2, early.base + len(early.spare))
        loop_base = second.base + len(second.spare)
        loop_uses = len(second.spare)
        LOOP_START, LOOP_END = 2, CHUNKS - 3

        def looped(i):
            return Segment(i, i + 1, (i - LOOP_START) * loop_uses + loop_base)

        peeled = Segment(LOOP_END, LOOP_END + 1, loop_base + (LOOP_END - LOOP_START) * loop_uses)
        late = Segment(CHUNKS - 2, CHUNKS - 1, peeled.base + len(peeled.spare), lead=STEPS + LEAD - steps_in(CHUNKS - 1), last=True)
        outro = Segment(CHUNKS - 1, None, late.base + len(late.spare))
        FINAL_USE = outro.base + len(outro.spare)

        def run(eng, segment):
            segment(intro)
            segment(early)
            segment(second)
            with eng.Fori(LOOP_START, LOOP_END) as i:
                segment(looped(i))
            segment(peeled)
            segment(late)
            segment(outro)

        comb_dram = nc.dram_tensor("comb_scratch", (CHUNKS, E * TOK), F32, kind="Internal").ap()

        def by_step(tile, c):
            return tile[:, 0:tokens(c)].rearrange("p (g t n) -> p g t n", t=GS, n=N)

        def by_group(tile, c):
            return tile[:, 0:tokens(c)].rearrange("p (t n g) -> p g t n", t=GS, n=N)

        def chunk_of(a, c):
            if steps_in(c) < STEPS:
                return a[:, first_step(c):first_step(c) + steps_in(c), :].rearrange("n (g t) d -> n g (t d)", t=GS)
            whole = a[:, STEPS // 2:T - STEPS // 2, :].rearrange("n (c g t) d -> c n g (t d)", g=NG, t=GS)
            return whole[c - 1]

        @block.sync
        def _(sp):
            def load_x(c):
                sp.dma_start(x_chunk[0:N * groups(c), :, :].rearrange("p t d -> p (t d)"), chunk_of(x, c)).then_inc(s_x, 16)

            def load_residual(c):
                sp.dma_start(x_res[0:N * groups(c), :, :].rearrange("p t d -> p (t d)"), chunk_of(x, c)).then_inc(s_res, 16)

            def store(c):
                sp.dma_start(chunk_of(out, c), out_sb[0:N * groups(c), :, :].rearrange("p t d -> p (t d)")).then_inc(s_out, 16)

            rows = [(ROW_B1, sb1.rearrange("(j p) -> j p", p=128)), (ROW_B1 + KT, eb1.rearrange("e (j p) -> (e j) p", p=128)),
                    (ROW_B2, sb2.rearrange("(a p) -> a p", a=1)), (ROW_B2 + 1, eb2),
                    (ROW_NW, nw.rearrange("(a p) -> a p", a=1)), (ROW_RW, rw)]
            sp.dma_start(given[0:N, :], cond).then_inc(s_given_in, 16)
            sp.dma_start(given[N:, :], b.rearrange("(g p) -> g p", p=128)).then_inc(s_given_in, 16)
            load_x(0)
            for r, src in rows:
                sp.dma_start(params_in[r:r + src.shape[0], :], src).then_inc(s_params_in, 16)

            def load_expert(n):
                w1, w2 = (sw1, sw2) if n == 0 else (ew1[n - 1], ew2[n - 1])
                sp.dma_start(w_raw[n % WRING][:, 0, :], w1).then_inc(s_w[n], 16)
                sp.dma_start(w_raw[n % WRING][:, 1, :].rearrange("p (j o) -> p j o", j=KT),
                             w2.rearrange("(j p) o -> p j o", p=128)).then_inc(s_w[n], 16)

            for n in range(WRING):
                load_expert(n)

            def segment(g):
                if not g.tail and not g.last:
                    sp.wait_ge(s_spare, g.use("x_first") + 1 if g.first else g.base)
                    load_x(g.lstm + 1)
                for l in g.steps:
                    if l == g.start + 1 and g.ffn is not None:
                        sp.wait_ge(s_spare_read, g.use("comb") + 1)
                        rows, half_width = E * groups(g.ffn), E // 2 * tokens(g.ffn)
                        sp.dma_start(comb_dram[g.ffn, 0:rows * 128].rearrange("(r t) -> r t", t=128), comb_rows[0:rows, :]).then_inc(s_row, 16)
                        sp.wait_ge(s_row, (g.ffn + 1) * 16)
                        for half in range(2):
                            wait(sp, s_wt, g.ffn * X - (0 if half else E // 2))
                            part = slice(half * half_width, (half + 1) * half_width)
                            sp.dma_start(comb_bc[:, part], comb_dram[g.ffn, part].partition_broadcast(128)
                                         ).then_inc(s_bc[half], 16)
                    if l == g.start + 3 and g.ffn is not None:
                        if g.has_final:
                            sp.wait_ge(s_spare_read, g.use("final") + 1)
                            store(g.ffn - 1)
                        load_residual(g.ffn)
                    n = WRING + l
                    if g.first and n < X:
                        sp.wait_ge(s_w1_split, n - WRING + 1)
                        sp.wait_ge(s_w2_split, n - WRING + 1)
                        load_expert(n)

            run(sp, segment)
            sp.wait_ge(s_spare_read, FINAL_USE + 1)
            store(CHUNKS - 1)
            sp.wait_ge(s_out, 16 * CHUNKS)

        @block.gpsimd
        def _(pool):
            count = [0]

            def ordered(ins):
                count[0] += 1
                ins.then_inc(s_const_step, 1)
                pool.wait_ge(s_const_step, count[0])

            nc.gpsimd.memset(opener[:, :], 0.0).then_inc(s_consts, 1)
            ordered(nc.gpsimd.memset(ident[:, :], 0.0))
            nc.gpsimd.affine_select(out=ident[:, :], in_=ident[:, :], compare_op=ALU.not_equal, fill=1.0, base=0,
                                    pattern=[[-1, 128]], channel_multiplier=1).then_inc(s_consts, 1)
            nc.gpsimd.memset(ones[:, :], 1.0)
            nc.gpsimd.memset(eps_top[:, :], EPS_TOP)
            nc.gpsimd.memset(minus_one[:, :], -1.0)
            ordered(nc.gpsimd.memset(before[:, :, :], 1.0))
            ordered(nc.gpsimd.affine_select(out=before[:, :, :], in_=before[:, :, :], compare_op=ALU.is_gt,
                                            fill=0.0, base=0, pattern=[[1, E], [-1, E]], channel_multiplier=0))
            nc.gpsimd.memset(minus_half[:, :], -0.5).then_inc(s_consts, 1)
            pool.wait_ge(s_consts, 3)

            def low_parts(c, tiles):
                for j in tiles:
                    if lo_on_pool(c, j):
                        pool.wait_ge(s_hf, c * TILES + j + 1)
                        nc.gpsimd.tensor_tensor(h_lo[j % RING][:, 0:tokens(c)], h_full[j % RING][:, 0:tokens(c)],
                                                h_hi[j % RING][:, 0:tokens(c)].bitcast(F32), ALU.subtract).then_inc(s_pool_lo, 1)

            def segment(g):
                for l in g.steps:
                    low_parts(g.ffn, g.taken_on(l))
                    if g.first and l < X:
                        pool.wait_ge(s_w_hi, 2 * l + 2)
                        nc.gpsimd.tensor_tensor(w_lo[:, l, 1, :], w_raw[l % WRING][:, 1, :], w_hi[:, l, 1, :].bitcast(F32), ALU.subtract).then_inc(s_w2_split, 1)
                    if l == g.take_stats_at:
                        pool.wait_ge(s_var, g.lstm + 1)
                        ng = groups(g.lstm)
                        nc.gpsimd.tensor_tensor(rms[:, 0:ng], var[:, 0:ng], minus_half[:, 0:ng], ALU.pow).then_inc(s_rms, 1)
                        pool.wait_ge(s_rms, g.lstm + 1)
                        pool.wait_ge(s_raw, g.lstm + 1)
                        nc.gpsimd.tensor_tensor(logits[:, 0:ng, :], raw_logits[:, 0:ng, :],
                                                rms[:, 0:ng].unsqueeze(2).broadcast_to([128, ng, E]), ALU.mult).then_inc(s_logits, 1)
                    if l == g.start and g.ffn is not None:
                        pool.wait_ge(s_total, g.ffn + 1)
                        ng = groups(g.ffn)
                        nc.gpsimd.tensor_tensor(total_eps[:, 0:ng], total[:, 0:ng], eps_top[:, 0:ng], ALU.add).then_inc(s_norm, 1)
                        pool.wait_ge(s_norm, g.ffn * 2 + 1)
                        nc.gpsimd.tensor_tensor(total_inv[:, 0:ng], total_eps[:, 0:ng], minus_one[:, 0:ng], ALU.pow).then_inc(s_norm, 1)
                        pool.wait_ge(s_norm, g.ffn * 2 + 2)
                        nc.gpsimd.tensor_tensor(comb[:, 0:E * ng].rearrange("p (e g) -> p g e", e=E), chosen[:, 0:ng, :],
                                                total_inv[:, 0:ng].unsqueeze(2).broadcast_to([128, ng, E]), ALU.mult).then_inc(s_comb, 1)
                    for n in g.weighed_at(l):
                        if n > 0:
                            pool.wait_ge(s_wt, g.ffn * X + n + 1)
                            wait(pool, s_acc, g.ffn * E + n - 1)
                            width = tokens(g.ffn)
                            nc.gpsimd.tensor_tensor(acc[:, 0:width], acc[:, 0:width], weighted[n % 2][:, 0:width], ALU.add).then_inc(s_acc, 1)
                    if g.opens(l):
                        pool.wait_ge(s_route, g.lstm * ROUTE + 2)
                        ng = groups(g.lstm)
                        nc.gpsimd.tensor_tensor(equal[:, 0:ng, :, :], equal[:, 0:ng, :, :],
                                                before[:, :, :].unsqueeze(1).broadcast_to([128, ng, E, E]), ALU.mult).then_inc(s_masked, 1)
                        pool.wait_ge(s_masked, g.lstm * 2 + 1)
                        nc.gpsimd.tensor_tensor(above[:, 0:ng, :, :], above[:, 0:ng, :, :], equal[:, 0:ng, :, :], ALU.add).then_inc(s_masked, 1)
                    if l == g.end - 1 and g.ffn is not None and not g.tail:
                        pool.wait_ge(s_wt, (g.ffn + 1) * X)
                        pool.wait_ge(s_acc, (g.ffn + 1) * E - 1)
                        if g.has_final:
                            pool.wait_ge(s_spare, g.use("final") + 1)
                        nc.gpsimd.tensor_tensor(by_group(summed, g.ffn), by_step(acc, g.ffn), by_step(weighted[(X - 1) % 2], g.ffn), ALU.add).then_inc(s_acc, 1)
                    if g.opens(l):
                        low_parts(g.lstm, range(2))

            run(pool, segment)

        @block.scalar
        def _(act):
            act.dma_start(wh_raw[:, :], Wh).then_inc(s_wh_in, 16)
            act.dma_start(wx_raw[:, :], Wx).then_inc(s_wx_in, 16)
            act.wait_ge(s_consts, 2)
            nc.scalar.mul(gates[0][:, GATES, :], ident[:, 0:N], 0.0).then_inc(s_zero_c, 1)

            def evacuate_x(c, use):
                act.wait_ge(s_spare, use + 1)
                nc.scalar.copy(by_step(x_t, c), by_group(spare_ps, c)).then_inc(s_spare_read, 1)

            def start_gates(group):
                nc.scalar.copy(gate_ps[group % 2][:, :].rearrange("p (g c) -> p g c", g=GATES),
                               b_cols[:, :].unsqueeze(2).broadcast_to([128, GATES, 128])).then_inc(s_bias, 1)

            evacuate_x(0, intro.use("x_first"))
            act.wait_ge(s_wx_in, 16)
            act.wait_ge(s_unit, UNITS)
            S = (GATES - 1) * D
            nc.scalar.mul(wx[:, 0:S], wx_raw[:, 0:S], unit[:, UNIT_WX_HALF:UNIT_WX_HALF + 1])
            nc.scalar.mul(wx[:, S:], wx_raw[:, S:], unit[:, UNIT_WX:UNIT_WX + 1]).then_inc(s_wx, 1)

            act.wait_ge(s_opened, 1)
            act.wait_ge(s_bcols, 1)
            start_gates(0)

            def squares(g, k):
                act.wait_ge(s_hs, g.step(GS * (k + 1)))
                if k == 0 and not g.first:
                    act.wait_ge(s_copied, g.lstm)
                cols = slice(k * 128, (k + 1) * 128)
                nc.scalar.activation(h_sq[:, cols], hs[:, cols], ACT.Square).then_inc(s_sq, 1)

            def relu(c, j):
                J, width = c * TILES + j, tokens(c)
                act.wait_ge(s_z, J + 1)
                wait(act, s_l2, J - RING + 1)
                bias = params[:, ROW_B1 + j:ROW_B1 + j + 1]
                if j % 2 == 0:
                    nc.scalar.activation(h_hi[j % RING][:, 0:width], z_ps[j % ZB][:, 0:width], ACT.Relu, bias=bias)
                nc.scalar.activation(h_full[j % RING][:, 0:width], z_ps[j % ZB][:, 0:width], ACT.Relu, bias=bias).then_inc(s_hf, 1)

            def segment(g):
                for l in g.steps:
                    if g.has_step(l):
                        s = g.step(l)
                        act.wait_ge(s_gates, s + 1)
                        nc.scalar.activation(gates[l % 2][:, 0:GATES, :],
                                             gate_ps[(l // GS) % 2][:, :].rearrange("p (g t n) -> p g t n", g=GATES, n=N)[:, :, l % GS, :],
                                             ACT.Tanh, scale=unit[:, UNIT_TANH:UNIT_TANH + 1]).then_inc(s_gates_act, 1)
                    if not g.tail and l in g.squares_at:
                        squares(g, g.squares_at.index(l))
                    if g.starts_gates(l):
                        start_gates(l // GS + 1)
                    for j in g.beside(l):
                        relu(g.ffn, j)
                    if g.opens(l) and not g.first:
                        relu(g.lstm, 0)
                    if g.has_step(l):
                        act.wait_ge(s_c, s + 1)
                        nc.scalar.activation(tanh_c[:, :], gates[(l + 1) % 2][:, GATES, :], ACT.Tanh, scale=0.5).then_inc(s_tanh_c, 1)
                    if g.first and l < X:
                        act.wait_ge(s_w[l], 32)
                        for w in range(2):
                            nc.scalar.copy(w_hi[:, l, w, :], w_raw[l % WRING][:, w, :]).then_inc(s_w_hi, 1)
                    if g.transposes_x(l):
                        evacuate_x(g.lstm + 1, g.use("x_next"))
                    for j in g.taken_on(l):
                        relu(g.ffn, j)
                    if l == g.scale_at:
                        act.wait_ge(s_logits, g.lstm + 1)
                        nc.scalar.activation(probs[:, 0:groups(g.lstm), :], logits[:, 0:groups(g.lstm), :], ACT.Sigmoid).then_inc(s_probs, 1)
                    if g.opens(l):
                        for j in range(0 if g.first else 1, 2):
                            relu(g.lstm, j)

            run(act, segment)

        @block.vector
        def _(dve):
            def chain(sem):
                n = [0]

                def step(ins):
                    n[0] += 1
                    ins.then_inc(sem, 1)
                    dve.wait_ge(sem, n[0])
                    return n[0]
                return step

            S = (GATES - 1) * D
            dve.wait_ge(s_wh_in, 16)
            nc.vector.tensor_reduce(row_max[:, :], wh_raw[:, :], AX.X, ALU.max, apply_absolute_value=True).then_inc(s_row_max, 1)
            dve.wait_ge(s_setup_ps, 1)
            scale = chain(s_unit)
            scale(nc.vector.tensor_reduce(wh_max[:, :], eo_ps[0][:, 0:128], AX.X, ALU.max))
            scale(nc.vector.tensor_scalar(row_max[:, :], wh_max[:, :], WH_LEAST, None, ALU.max))
            scale(nc.vector.tensor_scalar(wh_top[:, :].bitcast(I32), row_max[:, :].bitcast(I32), 0x7F800000, None, ALU.bitwise_and))
            scale(nc.vector.reciprocal(wh_top_inv[:, :], wh_top[:, :]))
            for column, factor in ((UNIT_WH, WH_SCALE), (UNIT_WH_HALF, WH_SCALE / 2), (UNIT_WX, WH_SCALE * H_SCALE),
                                   (UNIT_WX_HALF, WH_SCALE * H_SCALE / 2)):
                nc.vector.tensor_scalar(unit[:, column:column + 1], wh_top_inv[:, :], factor, None, ALU.mult).then_inc(s_unit, 1)
            nc.vector.tensor_scalar(unit[:, UNIT_TANH:UNIT_TANH + 1], wh_top[:, :], 1.0 / (WH_SCALE * H_SCALE), None, ALU.mult).then_inc(s_unit, 1)
            dve.wait_ge(s_unit, UNITS)
            dve.wait_ge(s_setup_ps, 2)
            nc.vector.tensor_scalar(b_cols[:, 0:GATES - 1], eo_ps[1][:, N:N + GATES - 1], unit[:, UNIT_WX_HALF:UNIT_WX_HALF + 1], None, ALU.mult)
            nc.vector.tensor_scalar(b_cols[:, GATES - 1:], eo_ps[1][:, N + GATES - 1:N + GATES], unit[:, UNIT_WX:UNIT_WX + 1], None, ALU.mult).then_inc(s_bcols, 1)
            param_step = chain(s_params)
            wh_step = chain(s_wh)
            nc.vector.tensor_scalar(wh[:, 0:S], wh_raw[:, 0:S], unit[:, UNIT_WH_HALF:UNIT_WH_HALF + 1], None, ALU.mult)
            wh_step(nc.vector.tensor_scalar(wh[:, S:], wh_raw[:, S:], unit[:, UNIT_WH:UNIT_WH + 1], None, ALU.mult))
            nc.vector.tensor_scalar(h_init[:, :], eo_ps[1][:, 0:N], H_SCALE, None, ALU.mult).then_inc(s_given, 1)
            dve.wait_ge(s_wh, 1)
            wh_step(nc.vector.tensor_copy(wh_parts[:, 0, :], wh[:, :]))
            nc.vector.tensor_tensor(wh_parts[:, 1, :], wh[:, :], wh_parts[:, 0, :], ALU.subtract).then_inc(s_wh, 1)

            def prepare_params(l):
                if l == 1:
                    dve.wait_ge(s_spare, intro.use("params") + 1)
                    nc.vector.tensor_copy(params[:, :], spare_ps[:, 0:ROWS]).then_inc(s_spare_read, 1)
                    dve.wait_ge(s_spare_read, intro.use("params") + 1)
                    param_step(nc.vector.tensor_scalar(nw_scaled[:, :], params[:, ROW_NW:ROW_NW + 1], 1.0 / H_SCALE, None, ALU.mult))
                if l == 2:
                    param_step(nc.vector.tensor_scalar(rw_scaled[:, :], params[:, ROW_RW:ROW_RW + E], nw_scaled[:, 0:1], None, ALU.mult))
                    param_step(nc.vector.tensor_copy(rw_parts[:, 0, :], rw_scaled[:, :]))
                if l == 3:
                    param_step(nc.vector.tensor_tensor(rw_rest[:, 0, :], rw_scaled[:, :], rw_parts[:, 0, :], ALU.subtract))
                    param_step(nc.vector.tensor_copy(rw_parts[:, 1, :], rw_rest[:, 0, :]))
                if l == 4:
                    param_step(nc.vector.tensor_tensor(rw_rest[:, 1, :], rw_rest[:, 0, :], rw_parts[:, 1, :], ALU.subtract))
                    last = param_step(nc.vector.tensor_copy(rw_parts[:, 2, :], rw_rest[:, 1, :]))
                    assert last == PARAM_STEPS

            def split(c, j):
                J, width = c * TILES + j, tokens(c)
                if lo_on_pool(c, j):
                    return
                dve.wait_ge(s_hf, J + 1)
                if j % 2:
                    nc.vector.tensor_copy(h_hi[j % RING][:, 0:width], h_full[j % RING][:, 0:width]).then_inc(s_hi, 1)
                    dve.wait_ge(s_hi, c * (TILES // 2) + j // 2 + 1)
                nc.vector.tensor_tensor(h_lo[j % RING][:, 0:width], h_full[j % RING][:, 0:width],
                                        h_hi[j % RING][:, 0:width].bitcast(F32), ALU.subtract).then_inc(s_lo, 1)

            def weigh(c, n):
                dve.wait_ge(s_l2, c * TILES + (n + 1) * KT)
                width = tokens(c)
                b2 = params[:, ROW_B2 + n:ROW_B2 + n + 1]
                if n == 0:
                    wait(dve, s_acc, c * E)
                    nc.vector.tensor_scalar(acc[:, 0:width], eo_ps[0][:, 0:width], b2, None, ALU.add).then_inc(s_wt, 1)
                else:
                    dve.wait_ge(s_bc[(n - 1) // (E // 2)], (c + 1) * 16)
                    wait(dve, s_acc, c * E + n - 2)
                    nc.vector.scalar_tensor_tensor(weighted[n % 2][:, 0:width], eo_ps[n % 2][:, 0:width], b2,
                                                   comb_bc[:, (n - 1) * width:n * width],
                                                   ALU.add, ALU.mult).then_inc(s_wt, 1)

            def final(ffn, use):
                dve.wait_ge(s_spare, use + 1)
                dve.wait_ge(s_res, 16 * (ffn + 1))
                wait(dve, s_out, 16 * ffn)
                rows = N * groups(ffn)
                nc.vector.tensor_tensor(out_sb[0:rows, :, :], spare_ps[0:rows, :].rearrange("p (t d) -> p t d", t=GS),
                                        x_res[0:rows, :, :], ALU.add).then_inc(s_spare_read, 1)

            def split_xn(g):
                c = g.lstm
                dve.wait_ge(s_spare_read, g.use("scale") + 1)
                wait(dve, s_z, c * TILES)
                nc.vector.tensor_copy(xn_hi[:, 0:tokens(c)], xn[:, 0:tokens(c)]).then_inc(s_xhi, 1)
                dve.wait_ge(s_xhi, c + 1)
                nc.vector.tensor_tensor(xn_lo[:, 0:tokens(c)], xn[:, 0:tokens(c)], xn_hi[:, 0:tokens(c)].bitcast(F32), ALU.subtract).then_inc(s_xlo, 1)

            def compare(c):
                dve.wait_ge(s_probs, c + 1)
                ng = groups(c)
                other = probs[:, 0:ng, :].unsqueeze(2).broadcast_to([128, ng, E, E])
                own = probs[:, 0:ng, :].unsqueeze(3).broadcast_to([128, ng, E, E])
                nc.vector.tensor_tensor(above[:, 0:ng, :, :], other, own, ALU.is_gt).then_inc(s_route, 1)
                nc.vector.tensor_tensor(equal[:, 0:ng, :, :], other, own, ALU.is_equal).then_inc(s_route, 1)

            def rank_probs(c):
                dve.wait_ge(s_masked, (c + 1) * 2)
                nc.vector.tensor_reduce(rank[:, 0:groups(c), :], above[:, 0:groups(c), :, :], AX.X, ALU.add).then_inc(s_route, 1)

            def choose(c):
                dve.wait_ge(s_route, c * ROUTE + 3)
                ng = groups(c)
                nc.vector.scalar_tensor_tensor(chosen[:, 0:ng, :], rank[:, 0:ng, :], 1.5, probs[:, 0:ng, :], ALU.is_lt, ALU.mult).then_inc(s_route, 1)
                dve.wait_ge(s_route, (c + 1) * ROUTE)
                nc.vector.tensor_reduce(total[:, 0:ng], chosen[:, 0:ng, :], AX.X, ALU.add).then_inc(s_total, 1)

            def take_spare(g, l):
                if l == g.take_stats_at:
                    dve.wait_ge(s_spare, g.use("stats") + 1)
                    ng = groups(g.lstm)
                    nc.vector.tensor_copy(stats[:, 0:ng, :], spare_ps[:, 0:ng * (1 + 3 * E)].rearrange("p (g k) -> p g k", g=ng)).then_inc(s_spare_read, 1)
                    dve.wait_ge(s_spare_read, g.use("stats") + 1)
                    nc.vector.tensor_scalar(var[:, 0:ng], stats[:, 0:ng, 0], 1.0 / (D * H_SCALE * H_SCALE), EPS_RMS, ALU.mult, ALU.add).then_inc(s_var, 1)
                    nc.vector.tensor_reduce(raw_logits[:, 0:ng, :], stats[:, 0:ng, 1:].rearrange("p g (k e) -> p g e k", k=3),
                                            AX.X, ALU.add).then_inc(s_raw, 1)
                if l == g.take_scale_at:
                    dve.wait_ge(s_spare, g.use("scale") + 1)
                    width = tokens(g.lstm)
                    nc.vector.scalar_tensor_tensor(xn[:, 0:width], hs[:, 0:width], nw_scaled[:, 0:1], spare_ps[:, 0:width], ALU.mult, ALU.mult).then_inc(s_spare_read, 1)

            def segment(g):
                for l in g.steps:
                    if not g.first:
                        take_spare(g, l)
                    if g.has_step(l):
                        s, now, nxt = g.step(l), gates[l % 2], gates[(l + 1) % 2]
                        dve.wait_ge(s_gates_act, s + 1)
                        if g.first and l == 0:
                            dve.wait_ge(s_zero_c, 1)
                        wait(dve, s_c, s)
                        nc.vector.scalar_tensor_tensor(uv[:, :, :], now[:, 0:2, :], 1.0, now[:, 3:5, :], ALU.add, ALU.mult).then_inc(s_uv, 1)
                        dve.wait_ge(s_uv, s + 1)
                        nc.vector.scalar_tensor_tensor(nxt[:, GATES, :], uv[:, 1, :], 0.5, uv[:, 0, :], ALU.mult, ALU.add).then_inc(s_c, 1)
                        nc.vector.tensor_scalar(o_scaled[:, :], now[:, 2, :], 1.0, H_SCALE / 2, ALU.add, ALU.mult).then_inc(s_o, 1)
                    if l == g.start and g.ffn is not None:
                        rank_probs(g.ffn)
                    for j in g.beside(l):
                        split(g.ffn, j)
                    if l == g.end - 1 and g.ffn is not None:
                        weigh(g.ffn, X - 1)
                    if g.opens(l) and not g.first:
                        compare(g.lstm)
                        split(g.lstm, 0)
                    if g.has_step(l):
                        dve.wait_ge(s_tanh_c, s + 1)
                        dve.wait_ge(s_o, s + 1)
                        cols = slice(l * N, (l + 1) * N)
                        nc.vector.tensor_tensor(h_a[:, cols], o_scaled[:, :], tanh_c[:, :], ALU.mult).then_inc(s_ha, 1)
                        nc.vector.tensor_tensor(hs[:, cols], o_scaled[:, :], tanh_c[:, :], ALU.mult).then_inc(s_hs, 1)
                        dve.wait_ge(s_hs, s + 1)
                        nc.vector.tensor_tensor(h_b[:, cols], hs[:, cols], h_a[:, cols], ALU.subtract).then_inc(s_h, 1)
                    if g.first:
                        take_spare(g, l)
                    if l == g.start + 3 and g.has_final:
                        final(g.ffn - 1, g.use("final"))
                    if g.first:
                        prepare_params(l)
                    if g.first and l < X:
                        dve.wait_ge(s_w_hi, 2 * l + 1)
                        nc.vector.tensor_tensor(w_lo[:, l, 0, :], w_raw[l % WRING][:, 0, :], w_hi[:, l, 0, :].bitcast(F32), ALU.subtract).then_inc(s_w1_split, 1)
                    if l == g.start + 1 and g.ffn is not None:
                        dve.wait_ge(s_spare, g.use("comb") + 1)
                        rows = E * groups(g.ffn)
                        nc.vector.tensor_copy(comb_rows[0:rows, :], spare_ps[0:rows, 0:128]).then_inc(s_spare_read, 1)
                    for j in g.taken_on(l):
                        split(g.ffn, j)
                    if l == g.split_xn_at:
                        split_xn(g)
                        if g.first:
                            compare(g.lstm)
                    if l == g.copy_at and not g.first and not g.tail:
                        dve.wait_ge(s_h, g.step(l))
                        for state in (h_a, h_b, hs):
                            last = nc.vector.tensor_copy(state[:, 0:g.start * N], state[:, tokens(g.ffn):tokens(g.ffn) + g.start * N])
                        last.then_inc(s_copied, 1)
                    if l == g.start and g.ffn is not None:
                        choose(g.ffn)
                    for n in g.weighed_at(l):
                        weigh(g.ffn, n)
                    if g.opens(l):
                        for j in range(0 if g.first else 1, 2):
                            split(g.lstm, j)

            run(dve, segment)
            dve.wait_ge(s_acc, CHUNKS * E - 1)
            dve.wait_ge(s_wt, CHUNKS * X)
            nc.vector.tensor_tensor(by_group(summed, CHUNKS - 1), by_step(acc, CHUNKS - 1),
                                    by_step(weighted[(X - 1) % 2], CHUNKS - 1), ALU.add).then_inc(s_acc, 1)
            final(CHUNKS - 1, FINAL_USE)

        @block.tensor
        def _(pe):
            def to_spare(g_use):
                wait(pe, s_spare_read, g_use)

            def transpose_x(c, use):
                pe.wait_ge(s_x, 16 * (c + 1))
                to_spare(use)
                rows = N * groups(c)
                for t in range(GS):
                    last = nc.tensor.transpose(spare_ps[:, t * rows:(t + 1) * rows], x_chunk[0:rows, t, :], ident[0:rows, 0:rows])
                last.then_inc(s_spare, 1)

            def prime(group, place, which):
                bank = gate_ps[group % 2]
                for k in which:
                    nc.tensor.matmul(bank[:, k * 128:(k + 1) * 128], wx[:, k * D:(k + 1) * D],
                                     x_t[:, place * 128:(place + 1) * 128], start=False, stop=False,
                                     skip_group_check=True)

            def lstm_step(g, l):
                s = g.step(l)
                bank = gate_ps[(l // GS) % 2]
                if g.first and l == 0:
                    pe.wait_ge(s_wh, 1)
                    pe.wait_ge(s_given, 1)
                    for k in range(GATES):
                        c0 = k * 128
                        last = nc.tensor.matmul(bank[:, c0:c0 + N], wh[:, k * D:(k + 1) * D], h_init[:, :], start=False, stop=False,
                                                skip_group_check=True)
                    last.then_inc(s_gates, 1)
                    return
                if g.first and l == 1:
                    pe.wait_ge(s_wh, WH_STEPS)
                prev = l - 1 if l > g.start else g.before - 1
                cols = slice(prev * N, (prev + 1) * N)
                wait(pe, s_ha, s)
                for h, parts in ((h_a, (0, 1)), (h_b, (0,))):
                    for k in range(GATES):
                        c0 = k * 128 + (l % GS) * N
                        for w in parts:
                            if h is h_b and k == 0 and w == 0:
                                wait(pe, s_h, s)
                            last = nc.tensor.matmul(bank[:, c0:c0 + N], wh_parts[:, w, k * D:(k + 1) * D], h[:, cols], start=False,
                                                    stop=(l % GS == GS - 1), skip_group_check=True)
                last.then_inc(s_gates, 1)

            def layer1(c, j):
                J, width = c * TILES + j, tokens(c)
                n, k = j // KT, j % KT
                if j == 0:
                    pe.wait_ge(s_xlo, c + 1)
                wait(pe, s_hf, J - ZB + 1)
                if isinstance(c, int) and c == 0 and k == 0:
                    pe.wait_ge(s_w1_split, n + 1)
                z, cols = z_ps[j % ZB][:, 0:width], slice(k * 128, (k + 1) * 128)
                nc.tensor.matmul(z, w_hi[:, n, 0, cols], xn_hi[:, 0:width], start=True, stop=False)
                nc.tensor.matmul(z, w_lo[:, n, 0, cols], xn_hi[:, 0:width], start=False, stop=False)
                nc.tensor.matmul(z, w_hi[:, n, 0, cols], xn_lo[:, 0:width], start=False, stop=True).then_inc(s_z, 1)

            def layer2(g, j):
                J, width = g.ffn * TILES + j, tokens(g.ffn)
                n, k = j // KT, j % KT
                if lo_on_pool(g.ffn, j):
                    pe.wait_ge(s_pool_lo, POOL_LO.index(j) + 1)
                else:
                    pe.wait_ge(s_lo, lo_done(g.ffn, j))
                if k == 0:
                    wait(pe, s_wt, g.ffn * X + (n - 1 if n else 0))
                if isinstance(g.ffn, int) and g.ffn == 0 and k == 0:
                    pe.wait_ge(s_w2_split, n + 1)
                eo, cols = eo_ps[n % 2][:, 0:width], slice(k * 128, (k + 1) * 128)
                nc.tensor.matmul(eo, w_hi[:, n, 1, cols], h_hi[j % RING][:, 0:width], start=(k == 0), stop=False)
                nc.tensor.matmul(eo, w_lo[:, n, 1, cols], h_hi[j % RING][:, 0:width], start=False, stop=False)
                nc.tensor.matmul(eo, w_hi[:, n, 1, cols], h_lo[j % RING][:, 0:width], start=False, stop=(k == KT - 1)).then_inc(s_l2, 1)

            def broadcast_columns(src, n):
                for k in range(n):
                    last = nc.tensor.transpose(spare_ps[:, k * 128:(k + 1) * 128], src(k).broadcast_to([128, 128]), ident[:, :])
                last.then_inc(s_spare, 1)

            def final(ffn, use):
                pe.wait_ge(s_acc, E * (ffn + 1))
                to_spare(use)
                rows = N * groups(ffn)
                for k in range(GS):
                    last = nc.tensor.transpose(spare_ps[0:rows, k * 128:(k + 1) * 128], summed[:, k * rows:(k + 1) * rows], ident[:, :])
                last.then_inc(s_spare, 1)

            def segment(g):
                if g.first:
                    pe.wait_ge(s_consts, 1)
                    for bank in gate_ps:
                        last = nc.tensor.matmul(bank[:, :], opener[:, 0:128], opener[:, :], start=True, stop=True)
                    last.then_inc(s_opened, 1)
                    pe.wait_ge(s_consts, 2)
                    pe.wait_ge(s_row_max, 1)
                    nc.tensor.transpose(eo_ps[0][:, 0:128], row_max[:, 0:1].broadcast_to([128, 128]), ident[:, :]).then_inc(s_setup_ps, 1)
                    pe.wait_ge(s_given_in, 32)
                    nc.tensor.transpose(eo_ps[1][:, 0:N + GATES], given[:, :], ident[0:N + GATES, 0:N + GATES]).then_inc(s_setup_ps, 1)
                    transpose_x(0, g.use("x_first"))
                    pe.wait_ge(s_wx, 1)
                    pe.wait_ge(s_bias, 1)
                    wait(pe, s_spare_read, g.use("x_first") + 1)
                    prime(0, 0, range(GATES))
                for l in g.steps:
                    if g.has_step(l):
                        lstm_step(g, l)
                    if g.first and l == 0:
                        pe.wait_ge(s_params_in, 6 * 16)
                        to_spare(g.use("params"))
                        nc.tensor.transpose(spare_ps[:, 0:ROWS], params_in[:, :], ident[0:ROWS, 0:ROWS]).then_inc(s_spare, 1)
                    if g.transposes_x(l):
                        transpose_x(g.lstm + 1, g.use("x_next"))
                    if g.primes(l):
                        if l == g.size - GS + 2:
                            wait(pe, s_spare_read, g.use("x_next") + 1)
                        if l % GS == 2:
                            pe.wait_ge(s_bias, first_group(g.lstm) + l // GS + 2)
                        k, which = g.primes(l)
                        prime(k, k if k < groups(g.lstm) else k - groups(g.lstm), which)
                    if l == g.start + 3 and g.has_final:
                        final(g.ffn - 1, g.use("final"))
                    for j in g.tiles_at(l):
                        if OPEN <= j + LAG < TILES:
                            layer1(g.ffn, j + LAG)
                        layer2(g, j)
                    if l == g.start + 1 and g.ffn is not None:
                        pe.wait_ge(s_comb, g.ffn + 1)
                        to_spare(g.use("comb"))
                        nc.tensor.transpose(spare_ps[0:E * groups(g.ffn), 0:128], comb[:, 0:E * groups(g.ffn)], ident[:, :]).then_inc(s_spare, 1)
                    if l == g.stats_at:
                        pe.wait_ge(s_sq, first_group(g.lstm) + groups(g.lstm))
                        if g.first:
                            pe.wait_ge(s_consts, 3)
                            pe.wait_ge(s_params, PARAM_STEPS)
                        to_spare(g.use("stats"))
                        for q in range(groups(g.lstm)):
                            cols, c0 = slice(q * 128, (q + 1) * 128), q * (1 + 3 * E)
                            nc.tensor.matmul(spare_ps[:, c0:c0 + 1], h_sq[:, cols], ones[:, :], start=True, stop=True)
                            parts = rw_parts[:, :, :].rearrange("p k e -> p (k e)")
                            nc.tensor.matmul(spare_ps[:, c0 + 1:c0 + 1 + 3 * E], h_a[:, cols], parts, start=True, stop=False)
                            last = nc.tensor.matmul(spare_ps[:, c0 + 1:c0 + 1 + 3 * E], h_b[:, cols], parts, start=False, stop=True)
                        last.then_inc(s_spare, 1)
                    if l == g.scale_at:
                        pe.wait_ge(s_rms, g.lstm + 1)
                        to_spare(g.use("scale"))
                        broadcast_columns(lambda k: rms[:, k:k + 1], groups(g.lstm))
                    if g.opens(l):
                        for j in range(OPEN):
                            layer1(g.lstm, j)

            run(pe, segment)
            final(CHUNKS - 1, FINAL_USE)


_INS = ['x', 'cond_1024', 'L0_cond_Wx', 'L0_cond_Wh', 'L0_cond_b', 'L0_ffn_norm_weight', 'L0_ffn_router_w', 'L0_ffn_sw1',
        'L0_ffn_sb1', 'L0_ffn_sw2', 'L0_ffn_sb2', 'L0_ffn_ew1', 'L0_ffn_eb1', 'L0_ffn_ew2', 'L0_ffn_eb2']
_OUTS = [((N, T, D), 'float32')]


def kernel(**inputs):
    import numpy as _np
    import concourse.bacc as _bacc
    from concourse import mybir as _mybir
    from concourse.bass_utils import run_bass_kernel_spmd as _run

    nc = _bacc.Bacc("TRN2", target_bir_lowering=False, num_devices=1)
    arrays, args = {}, []
    for name in _INS:
        a = _np.ascontiguousarray(inputs[name])
        arrays[f"in_{name}_dram"] = a
        args.append(nc.dram_tensor(f"in_{name}_dram", a.shape, _mybir.dt.from_np(a.dtype), kind="ExternalInput").ap())
    for i, (shape, dtype) in enumerate(_OUTS):
        dt = _mybir.dt.from_np(_np.dtype(dtype))
        args.append(nc.dram_tensor(f"out_{i}_dram", shape, dt, kind="ExternalOutput").ap())
    adaln_ffn_kernel(nc, *args)
    r = _run(nc, [arrays], core_ids=[0])
    return r.results[0]["out_0_dram"]
```
